# Optimizing a Trainium2 kernel written in Bass

```python
import numpy as np
import jax
import jax.numpy as jnp

def _softmax(x, axis=-1):
    return jax.nn.softmax(x, axis=axis)

def _gelu(x):
    return jax.nn.gelu(x, approximate=True)

def _silu(x):
    return jax.nn.silu(x)

def _sigmoid(x):
    return jax.nn.sigmoid(x)

def _layernorm(x, axis=-1, eps=1e-05):
    m = jnp.mean(x, axis=axis, keepdims=True)
    v = jnp.var(x, axis=axis, keepdims=True)
    return (x - m) / jnp.sqrt(v + eps)

def _scatter_add(tgt, idx, src, axis=0):
    return tgt.at[idx].add(src)

def _segment_sum(src, seg, n):
    return jax.ops.segment_sum(src, seg, n)
kernel_name = 'mk_seq_postln_d1_jaxref_r8_97cdf3'

def setup_inputs(seed: int=0):
    np.random.seed(seed)
    _w = jnp.asarray

    def _L0_attn_setup():
        import jax, jax.numpy as jnp
        import numpy as np
        D = 128
        B, L = (4, 1024)
        EPS = 1e-06
        key = jax.random.key(seed)
        ks = jax.random.split(key, 5)
        scale = 0.02
        X = jax.random.normal(ks[0], (B, L, D), dtype=jnp.float32)
        Wq = jax.random.normal(ks[1], (D, D), dtype=jnp.float32) * scale
        Wk = jax.random.normal(ks[2], (D, D), dtype=jnp.float32) * scale
        Wv = jax.random.normal(ks[3], (D, D), dtype=jnp.float32) * scale
        Wc = jax.random.normal(ks[4], (D, D), dtype=jnp.float32) * scale
        return {'X': X, 'Wq': Wq, 'Wk': Wk, 'Wv': Wv, 'Wc': Wc}
    _L0_attn_in = _L0_attn_setup()

    def _L0_ffn_setup():
        import jax, jax.numpy as jnp
        import numpy as np
        B, S, D, F, E, TOP_K = (4, 256, 128, 512, 8, 2)
        LN_EPS = 1e-05
        key = jax.random.key(seed)
        ks = jax.random.split(key, 4)
        sc = lambda fan_in: 1.0 / np.sqrt(fan_in)
        return {'x': jax.random.normal(ks[0], (B, S, D), jnp.float32), 'W1': jax.random.normal(ks[1], (E, D, F), jnp.float32) * sc(D), 'b1': jnp.zeros((E, F), jnp.float32), 'W2': jax.random.normal(ks[2], (E, F, D), jnp.float32) * sc(F), 'b2': jnp.zeros((E, D), jnp.float32), 'Wr': jax.random.normal(ks[3], (D, E), jnp.float32) * sc(D), 'br': jnp.zeros((E,), jnp.float32), 'gamma': jnp.ones((D,), jnp.float32), 'beta': jnp.zeros((D,), jnp.float32)}
    _L0_ffn_in = _L0_ffn_setup()
    _d = {'L0_attn_X': _L0_attn_in['X'], 'L0_attn_Wq': _L0_attn_in['Wq'], 'L0_attn_Wk': _L0_attn_in['Wk'], 'L0_attn_Wv': _L0_attn_in['Wv'], 'L0_attn_Wc': _L0_attn_in['Wc'], 'L0_ffn_W1': _L0_ffn_in['W1'], 'L0_ffn_b1': _L0_ffn_in['b1'], 'L0_ffn_W2': _L0_ffn_in['W2'], 'L0_ffn_b2': _L0_ffn_in['b2'], 'L0_ffn_Wr': _L0_ffn_in['Wr'], 'L0_ffn_br': _L0_ffn_in['br'], 'L0_ffn_gamma': _L0_ffn_in['gamma'], 'L0_ffn_beta': _L0_ffn_in['beta']}
    _x0 = _d['L0_attn_X']
    _d['L0_attn_X'] = jax.random.normal(jax.random.fold_in(jax.random.key(seed), 1), (8, 256, 128), dtype=_x0.dtype)
    del _x0
    return _d

def reference(L0_attn_X, L0_attn_Wq, L0_attn_Wk, L0_attn_Wv, L0_attn_Wc, L0_ffn_W1, L0_ffn_b1, L0_ffn_W2, L0_ffn_b2, L0_ffn_Wr, L0_ffn_br, L0_ffn_gamma, L0_ffn_beta):

    def _L0_attn_ref(X, Wq, Wk, Wv, Wc):
        import jax, jax.numpy as jnp
        import numpy as np
        D = 128
        B, L = (4, 1024)
        EPS = 1e-06
        V = jnp.einsum('bld,de->ble', X, Wv)
        K = jnp.exp(jnp.einsum('bld,de->ble', X, Wk))
        K_factor = jnp.cumsum(K, axis=1) + EPS
        S = jnp.cumsum(K * V, axis=1) / K_factor
        Q = jax.nn.sigmoid(jnp.einsum('bld,de->ble', X, Wq))
        O = S * Q
        return jnp.einsum('bld,de->ble', O, Wc)

    def _L0_ffn_ref(x, W1, b1, W2, b2, Wr, br, gamma, beta):
        import jax, jax.numpy as jnp
        import numpy as np
        B, S, D, F, E, TOP_K = (4, 256, 128, 512, 8, 2)
        LN_EPS = 1e-05
        b, s, d = x.shape
        e = Wr.shape[1]
        rw = jax.nn.softmax(x.mean(axis=1) @ Wr + br, axis=-1)
        x_flat = x.reshape(-1, d)
        rw_tok = jnp.repeat(rw, s, axis=0)
        tk_w, tk_i = jax.lax.top_k(rw_tok, TOP_K)
        tk_w = jax.nn.softmax(tk_w, axis=-1)
        h = jax.nn.gelu(jnp.einsum('nd,edf->enf', x_flat, W1) + b1[:, None, :], approximate=False)
        expert_out = jnp.einsum('enf,efd->end', h, W2) + b2[:, None, :]
        onehot = jax.nn.one_hot(tk_i, e, dtype=x.dtype)
        cw = jnp.einsum('nk,nke->ne', tk_w, onehot)
        out = jnp.einsum('ne,end->nd', cw, expert_out).reshape(b, s, d)
        y = out + x
        mu = y.mean(axis=-1, keepdims=True)
        var = y.var(axis=-1, keepdims=True)
        return (y - mu) / jnp.sqrt(var + LN_EPS) * gamma + beta
    x = L0_attn_X
    x = _layernorm(x + _L0_attn_ref(x, L0_attn_Wq, L0_attn_Wk, L0_attn_Wv, L0_attn_Wc), axis=-1)
    x = _layernorm(x + _L0_ffn_ref(x, L0_ffn_W1, L0_ffn_b1, L0_ffn_W2, L0_ffn_b2, L0_ffn_Wr, L0_ffn_br, L0_ffn_gamma, L0_ffn_beta), axis=-1)
    return x

_drawn_inputs = setup_inputs


def setup_inputs(seed=0):
    import zlib

    import numpy as np

    out = dict(_drawn_inputs(seed))
    spreads = {'L0_ffn_b1': (0.0, 0.341),
     'L0_ffn_b2': (0.0, 0.278),
     'L0_ffn_br': (0.0, 0.1),
     'L0_ffn_gamma': (1.0, 0.2),
     'L0_ffn_beta': (0.0, 0.1)}
    factors = {'L0_attn_Wq': 8.0, 'L0_attn_Wk': 8.0, 'L0_attn_Wv': 8.0, 'L0_attn_Wc': 8.0}
    for name, (base, spread) in spreads.items():
        noise = np.random.default_rng([zlib.crc32(name.encode()), seed]).standard_normal(out[name].shape)
        drawn = base * np.exp(spread * noise) if base else spread * noise
        out[name] = jnp.asarray(drawn.astype(out[name].dtype))
    for name, factor in factors.items():
        out[name] = (out[name] * factor).astype(out[name].dtype)
    return out
```

```python
import concourse.bass as bass
from concourse import mybir
from contextlib import ExitStack

F32 = mybir.dt.float32
U32 = mybir.dt.uint32
ALU = mybir.AluOpType
ACT = mybir.ActivationFunctionType
AX = mybir.AxisListType

ATTN_EPS = 1e-6
LN_EPS = 1e-5
TOP_K = 2


def attention_free_moe_block(nc, xt_d, x_d, wkvqc_d, w1b_d, w2_d, b2_d, wr_d, rows_d, ident_d, out_d):
    B, S, D = x_d.shape
    E = w1b_d.shape[0]
    NF = w2_d.shape[2] // D
    F = NF * D
    NT = S // 128
    GB = 512 // S
    G, GS = B // GB, GB * S
    AHEAD = 2
    assert D == 128 and S == 256 and B % 2 == 0 and B >= 4

    with ExitStack() as ctx:
        def sb(name, shape, dt=F32):
            return ctx.enter_context(nc.sbuf_tensor(name, shape, dt))

        def psum(name, shape, dt=F32):
            return ctx.enter_context(nc.psum_tensor(name, shape, dt))

        def sem(name):
            return ctx.enter_context(nc.semaphore(name))

        xt = sb("xt", [D, B * S])
        x_tok = sb("x_tok", [128, B * NT, D])
        wkvqc = sb("wkvqc", [D, 4 * D])
        wc_half = sb("wc_half", [D, D])
        wr = sb("wr", [D, E])
        rows = sb("rows", [128, E + 2 * D])
        ident = sb("ident", [128, 128])
        ones = sb("ones", [128, S])
        neg_half = sb("neg_half", [128, NT])
        br_row = rows[:, 0:E]
        gamma_row = rows[:, E:E + D]
        beta_row = rows[:, E + D:E + 2 * D]

        k_exp = sb("k_exp", [D, B * S])
        v_sb = sb("v_sb", [D, B * S])
        q_tanh = sb("q_tanh", [D, B * S])
        k_sum = [sb(f"k_sum{p}", [D, S]) for p in range(2)]
        k_inv = [sb(f"k_inv{p}", [D, S]) for p in range(2)]
        kv = [sb(f"kv{p}", [D, S]) for p in range(2)]
        kv_sum = [sb(f"kv_sum{p}", [D, S]) for p in range(2)]
        kv_gate = [sb(f"kv_gate{p}", [D, S]) for p in range(2)]
        o_t = [sb(f"o_t{p}", [D, S]) for p in range(2)]

        res1 = [sb(f"res1_{p}", [128, NT, D]) for p in range(2)]
        x1 = [sb(f"x1_{p}", [128, NT, D]) for p in range(2)]
        x1_t = [sb(f"x1_t{p}", [D, S]) for p in range(2)]
        x1_sum = [sb(f"x1_sum{p}", [D, 1]) for p in range(2)]
        logits = [sb(f"logits{p}", [128, E]) for p in range(2)]
        top = [sb(f"top{p}", [128, E]) for p in range(2)]
        top_i = [sb(f"top_i{p}", [128, E], U32) for p in range(2)]
        top_d = [sb(f"top_d{p}", [128, E]) for p in range(2)]
        th8 = [sb(f"th8_{p}", [128, E]) for p in range(2)]
        den8 = [sb(f"den8_{p}", [128, E]) for p in range(2)]
        inv8 = [sb(f"inv8_{p}", [128, E]) for p in range(2)]
        exp8 = [sb(f"exp8_{p}", [128, E]) for p in range(2)]
        sum8 = [sb(f"sum8_{p}", [128, 1]) for p in range(2)]
        isum8 = [sb(f"isum8_{p}", [128, 1]) for p in range(2)]
        dp = [sb(f"dp{p}", [128, 1]) for p in range(2)]
        th2 = [sb(f"th2_{p}", [128, 1]) for p in range(2)]
        w_top = [sb(f"w_top{p}", [128, TOP_K]) for p in range(2)]

        w1b = [sb(f"w1b{s}", [D, F + NF]) for s in range(2 * TOP_K)]
        w2 = [sb(f"w2_{s}", [128, NF, D]) for s in range(2 * TOP_K)]
        b2 = [sb(f"b2_{s}", [128, D]) for s in range(2 * TOP_K)]
        h_t = [sb(f"h_t{k}", [128, NF, S]) for k in range(TOP_K)]
        b2w = [sb(f"b2w{k}", [128, D]) for k in range(TOP_K)]
        b2c = sb("b2c", [128, D])
        x1_b2 = [sb(f"x1_b2_{p}", [128, NT, D]) for p in range(2)]
        x1_beta = [sb(f"x1_beta{p}", [128, NT, D]) for p in range(2)]
        y0 = sb("y0", [128, NT, D])
        y = sb("y", [128, NT, D])
        z = sb("z", [128, NT, D])
        zg = sb("zg", [128, NT, D])
        u = sb("u", [128, NT, D])
        fin = [sb(f"fin{p}", [128, NT, D]) for p in range(2)]

        stats = [sb(f"stats{n}", [128, NT, 6]) for n in range(3)]
        mv = [sb(f"mv{n}", [128, NT, 2]) for n in range(3)]
        var_eps = [sb(f"var_eps{n}", [128, NT]) for n in range(3)]
        rstd = [sb(f"rstd{n}", [128, NT]) for n in range(3)]
        shift = [sb(f"shift{n}", [128, NT]) for n in range(3)]

        bank = [psum(f"bank{n}", [128, 512]) for n in range(8)]
        kvq_ps = [bank[0:3], bank[5:8]]
        attn_ps = bank[3][:, 0:S]
        x1t_ps = bank[4][:, 0:S]
        logit_ps = bank[4][:, S:S + E]
        h_ps = [bank[0:2], bank[5:7]]
        out_ps = [bank[2], bank[7]]

        in_k = sem("in_k")
        in_xt = [sem(f"in_xt{n}") for n in range(G)]
        in_x = sem("in_x")
        in_small = sem("in_small")
        const_ok = sem("const_ok")
        wc_ok = sem("wc_ok")
        k_in_ps = sem("k_in_ps")
        v_in_ps = sem("v_in_ps")
        q_in_ps = sem("q_in_ps")
        k_exp_ok = sem("k_exp_ok")
        v_ok = sem("v_ok")
        q_tanh_ok = sem("q_tanh_ok")
        k_sum_ok = sem("k_sum_ok")
        k_inv_ok = sem("k_inv_ok")
        kv_ok = sem("kv_ok")
        kv_sum_ok = sem("kv_sum_ok")
        kv_gate_ok = sem("kv_gate_ok")
        o_t_ok = sem("o_t_ok")
        attn_in_ps = sem("attn_in_ps")
        res1_ok = sem("res1_ok")
        stats_ok = [sem(f"stats_ok{n}") for n in range(3)]
        mv_ok = [sem(f"mv_ok{n}") for n in range(3)]
        eps_ok = [sem(f"eps_ok{n}") for n in range(3)]
        rstd_ok = [sem(f"rstd_ok{n}") for n in range(3)]
        shift_ok = [sem(f"shift_ok{n}") for n in range(3)]
        x1_ok = sem("x1_ok")
        x1t_in_ps = sem("x1t_in_ps")
        x1_t_ok = sem("x1_t_ok")
        logit_in_ps = sem("logit_in_ps")
        logits_ok = sem("logits_ok")
        top_ok = sem("top_ok")
        top_i_ok = sem("top_i_ok")
        top_d_ok = sem("top_d_ok")
        th8_ok = sem("th8_ok")
        den8_ok = sem("den8_ok")
        inv8_ok = sem("inv8_ok")
        exp8_ok = sem("exp8_ok")
        sum8_ok = sem("sum8_ok")
        isum8_ok = sem("isum8_ok")
        dp_ok = sem("dp_ok")
        th2_ok = sem("th2_ok")
        w_top_ok = sem("w_top_ok")
        w1_in = [sem(f"w1_in{s}") for s in range(2 * TOP_K)]
        w2_in = [sem(f"w2_in{s}") for s in range(2 * TOP_K)]
        b2_in = [sem(f"b2_in{s}") for s in range(2 * TOP_K)]
        h_in_ps = sem("h_in_ps")
        h_ok = sem("h_ok")
        out_in_ps = sem("out_in_ps")
        b2w_ok = sem("b2w_ok")
        b2c_ok = sem("b2c_ok")
        x1_b2_ok = sem("x1_b2_ok")
        x1_beta_ok = sem("x1_beta_ok")
        y0_ok = sem("y0_ok")
        y_ok = sem("y_ok")
        z_ok = sem("z_ok")
        zg_ok = sem("zg_ok")
        u_ok = sem("u_ok")
        fin_ok = sem("fin_ok")
        out_dma = [sem(f"out_dma{p}") for p in range(2)]

        block = ctx.enter_context(nc.Block())

        @block.sync
        def _(sp):
            for g in range(G):
                sp.dma_start(xt[:, g * GS:(g + 1) * GS], xt_d[:, g * GS:(g + 1) * GS]).then_inc(in_xt[g], 16)

            def fetch(b, p, i):
                sp.wait_ge(top_i_ok, b + 1)
                for k in range(TOP_K):
                    s = TOP_K * p + k
                    e = sp.value_load(top_i[p][0:1, k:k + 1], min_val=0, max_val=E - 1)
                    if not (isinstance(b, int) and b < 2):
                        sp.wait_ge(out_in_ps, 2 * b - 3 + k)
                        sp.wait_ge(x1_b2_ok, b - 1)
                    sp.dma_start(w1b[s][:, :], w1b_d[bass.ds(e, 1), :, :].rearrange("e p n -> (e p) n")
                                 ).then_inc(w1_in[s], 16)
                    sp.dma_start(w2[s][:, :, :].rearrange("p c d -> p (c d)"),
                                 w2_d[bass.ds(e, 1), :, :].rearrange("e p n -> (e p) n")).then_inc(w2_in[s], 16)
                    sp.dma_start(b2[s][:, :], b2_d[bass.ds(e, 1), :].partition_broadcast(128)
                                 .rearrange("p e d -> p (e d)")).then_inc(b2_in[s], 16)

            def store(b, p):
                sp.wait_ge(fin_ok, b + 1)
                sp.dma_start(out_d[bass.ds(b, 1), :, :].rearrange("b (j t) d -> t (b j) d", t=128),
                             fin[p][:, :, :]).then_inc(out_dma[p], 16)

            for b in range(B):
                fetch(b, b % 2, b // 2)
                if b >= AHEAD + 1:
                    store(b - AHEAD - 1, (b - AHEAD - 1) % 2)
            for b in range(B - AHEAD - 1, B):
                store(b, b % 2)
            for p in range(2):
                sp.wait_ge(out_dma[p], 16 * (B // 2))

        @block.tensor
        def _(pe):
            def project(g):
                pe.wait_ge(in_xt[g], 16)
                cols = xt[:, g * GS:(g + 1) * GS]
                if g >= 2:
                    pe.wait_ge(k_exp_ok, g - 1)
                pe.matmul(kvq_ps[g % 2][0][:, :], wkvqc[:, 0:D], cols, start=True, stop=True).then_inc(k_in_ps, 1)
                if g >= 2:
                    pe.wait_ge(v_ok, g - 1)
                pe.matmul(kvq_ps[g % 2][1][:, :], wkvqc[:, D:2 * D], cols, start=True, stop=True).then_inc(v_in_ps, 1)
                if g >= 2:
                    pe.wait_ge(q_tanh_ok, g - 1)
                pe.matmul(kvq_ps[g % 2][2][:, :], wkvqc[:, 2 * D:3 * D], cols, start=True,
                          stop=True).then_inc(q_in_ps, 1)

            def attn_out(b, p):
                pe.wait_ge(o_t_ok, b + 1)
                if isinstance(b, int) and b == 0:
                    pe.wait_ge(wc_ok, 1)
                else:
                    pe.wait_ge(res1_ok, b)
                for t in range(NT):
                    mm = pe.matmul(attn_ps[:, t * D:(t + 1) * D], o_t[p][:, t * 128:(t + 1) * 128], wc_half[:, :],
                                   start=True, stop=True)
                mm.then_inc(attn_in_ps, 1)

            def transpose_x1(b, p):
                pe.wait_ge(x1_ok, b + 1)
                if isinstance(b, int) and b == 0:
                    pe.wait_ge(in_small, 48)
                else:
                    pe.wait_ge(logits_ok, b)
                for t in range(NT):
                    mm = pe.transpose(x1t_ps[:, t * 128:(t + 1) * 128], x1[p][:, t, :], ident[:, :])
                mm.then_inc(x1t_in_ps, 1)

            def router(b, p):
                pe.wait_ge(x1_t_ok, b + 1)
                pe.matmul(logit_ps, x1_sum[p][:, 0:1].to_broadcast([D, 128]), wr[:, :], start=True,
                          stop=True).then_inc(logit_in_ps, 1)

            def up(b, p, k, i):
                s = TOP_K * p + k
                pe.wait_ge(w1_in[s], 16 * (i + 1))
                if p == 0 and isinstance(i, int) and i == 0:
                    pe.wait_ge(v_ok, G - 1 + k)
                for c in range(NF):
                    mm = pe.matmul(h_ps[k][c // 2][:, (c % 2) * S:(c % 2 + 1) * S], w1b[s][:, c * D:(c + 1) * D],
                                   x1_t[p][:, :], start=True, stop=True)
                    if c % 2:
                        mm.then_inc(h_in_ps, 1)

            def down(b, p, k, i):
                s = TOP_K * p + k
                q = 2 * b + k
                pe.wait_ge(w2_in[s], 16 * (i + 1))
                pe.wait_ge(h_ok, q + 1)
                if k == 0 and not (isinstance(b, int) and b < 2):
                    pe.wait_ge(y_ok, b - 1)
                if k == 0 and isinstance(b, int) and b < 2:
                    pe.wait_ge(q_tanh_ok, G - 1 + b)
                for t in range(NT):
                    for c in range(NF):
                        mm = pe.matmul(out_ps[p][:, k * S + t * D:k * S + (t + 1) * D],
                                       h_t[k][:, c, t * 128:(t + 1) * 128], w2[s][:, c, :],
                                       start=(c == 0), stop=(c == NF - 1))
                mm.then_inc(out_in_ps, 1)

            pe.wait_ge(in_k, 16)
            project(0)
            project(1)
            attn_out(0, 0)
            project(2)
            transpose_x1(0, 0)
            attn_out(1, 1)
            router(0, 0)
            project(3)
            transpose_x1(1, 1)
            router(1, 1)
            up(0, 0, 0, 0)
            for b in range(B):
                p, i = b % 2, b // 2
                ahead = b + AHEAD < B
                if ahead:
                    attn_out(b + AHEAD, p)
                up(b, p, 1, i)
                down(b, p, 0, i)
                if ahead:
                    transpose_x1(b + AHEAD, p)
                if b + 1 < B:
                    up(b + 1, 1 - p, 0, (b + 1) // 2)
                if ahead:
                    router(b + AHEAD, p)
                down(b, p, 1, i)

        @block.scalar
        def _(act):
            act.dma_start(wkvqc[:, :], wkvqc_d).then_inc(in_k, 16)
            act.dma_start(wr[:, :], wr_d).then_inc(in_small, 16)
            act.dma_start(rows[:, :], rows_d.partition_broadcast(128)).then_inc(in_small, 16)
            act.dma_start(ident[:, :], ident_d).then_inc(in_small, 16)
            act.dma_start(x_tok[:, :, :], x_d.rearrange("b (j t) d -> t (b j) d", t=128)).then_inc(in_x, 16)

            def keys(g):
                cols = slice(g * GS, (g + 1) * GS)
                act.wait_ge(k_in_ps, g + 1)
                nc.scalar.activation(k_exp[:, cols], kvq_ps[g % 2][0][:, :], ACT.Exp).then_inc(k_exp_ok, 1)
                act.wait_ge(v_in_ps, g + 1)
                nc.scalar.copy(v_sb[:, cols], kvq_ps[g % 2][1][:, :]).then_inc(v_ok, 1)
                act.wait_ge(q_in_ps, g + 1)
                nc.scalar.activation(q_tanh[:, cols], kvq_ps[g % 2][2][:, :], ACT.Tanh,
                                     scale=0.5).then_inc(q_tanh_ok, 1)

            def norm(n, src, dst, b, done):
                act.wait_ge(shift_ok[n], b + 1)
                for t in range(NT):
                    a = nc.scalar.activation(dst[:, t, :], src[:, t, :], ACT.Identity, bias=shift[n][:, t:t + 1],
                                             scale=rstd[n][:, t:t + 1])
                a.then_inc(done, 1)

            def norm1(b, p):
                if not (isinstance(b, int) and b < 2):
                    act.wait_ge(x1_b2_ok, b - 1)
                    act.wait_ge(x1_beta_ok, b - 1)
                norm(0, res1[p], x1[p], b, x1_ok)

            def evacuate_x1t(b, p):
                act.wait_ge(x1t_in_ps, b + 1)
                nc.scalar.activation(x1_t[p][:, :], x1t_ps, ACT.Identity,
                                     accum_out=x1_sum[p][:, :]).then_inc(x1_t_ok, 1)

            def gelu(b, p, k):
                q = 2 * b + k
                for c in range(NF):
                    if c % 2 == 0:
                        act.wait_ge(h_in_ps, NF // 2 * q + c // 2 + 1)
                    if c == 0 and not (isinstance(b, int) and b < 1):
                        act.wait_ge(out_in_ps, q - 1)
                    a = nc.scalar.activation(h_t[k][:, c, :], h_ps[k][c // 2][:, (c % 2) * S:(c % 2 + 1) * S],
                                             ACT.Gelu, bias=w1b[TOP_K * p + k][:, F + c:F + c + 1])
                a.then_inc(h_ok, 1)

            def router_tanh8(b, p):
                act.wait_ge(top_d_ok, b + 1)
                nc.scalar.activation(th8[p][:, :], top_d[p][:, :], ACT.Tanh, scale=0.5).then_inc(th8_ok, 1)

            def router_tanh2(b, p):
                act.wait_ge(dp_ok, b + 1)
                nc.scalar.activation(th2[p][:, :], dp[p][:, :], ACT.Tanh, scale=0.5).then_inc(th2_ok, 1)

            def norm2(b):
                norm(1, y, z, b, z_ok)

            def norm3(b, p):
                if not (isinstance(b, int) and b < 2):
                    act.wait_ge(out_dma[p], 16 * ((b - p) // 2))
                norm(2, u, fin[p], b, fin_ok)

            keys(0)
            keys(1)
            norm1(0, 0)
            keys(2)
            evacuate_x1t(0, 0)
            norm1(1, 1)
            keys(3)
            evacuate_x1t(1, 1)
            router_tanh8(0, 0)
            router_tanh2(0, 0)
            router_tanh8(1, 1)
            gelu(0, 0, 0)
            for b in range(B + 1):
                p = b % 2
                ahead = b + AHEAD < B
                if b < B:
                    gelu(b, p, 1)
                if b + 1 < B:
                    router_tanh2(b + 1, 1 - p)
                if ahead:
                    norm1(b + AHEAD, p)
                if b > 0:
                    norm2(b - 1)
                if ahead:
                    evacuate_x1t(b + AHEAD, p)
                if b + 1 < B:
                    gelu(b + 1, 1 - p, 0)
                if b > 0:
                    norm3(b - 1, 1 - p)
                if ahead:
                    router_tanh8(b + AHEAD, p)

        @block.vector
        def _(dve):
            nc.vector.memset(ones[:, :], 1.0).then_inc(const_ok, 1)
            nc.vector.memset(neg_half[:, :], -0.5).then_inc(const_ok, 1)
            dve.wait_ge(in_k, 16)
            nc.vector.tensor_scalar(wc_half[:, :], wkvqc[:, 3 * D:4 * D], 0.5, None, ALU.mult).then_inc(wc_ok, 1)

            def cols(a, b):
                return a[:, bass.ds(b * S, S)]

            def group(b):
                return min(b // GB, G - 1) if isinstance(b, int) else b // GB

            def attn_denominator(b, p):
                dve.wait_ge(k_exp_ok, group(b) + 1)
                nc.vector.tensor_tensor_scan(k_sum[p][:, :], ones[:, :], cols(k_exp, b), ATTN_EPS, ALU.mult,
                                             ALU.add).then_inc(k_sum_ok, 1)
                dve.wait_ge(k_sum_ok, b + 1)
                nc.vector.reciprocal(k_inv[p][:, :], k_sum[p][:, :]).then_inc(k_inv_ok, 1)

            def attn_numerator(b, p):
                dve.wait_ge(v_ok, group(b) + 1)
                nc.vector.tensor_tensor(kv[p][:, :], cols(k_exp, b), cols(v_sb, b), ALU.mult).then_inc(kv_ok, 1)
                dve.wait_ge(kv_ok, b + 1)
                nc.vector.tensor_tensor_scan(kv_sum[p][:, :], ones[:, :], kv[p][:, :], 0.0, ALU.mult,
                                             ALU.add).then_inc(kv_sum_ok, 1)
                dve.wait_ge(q_tanh_ok, group(b) + 1)
                dve.wait_ge(kv_sum_ok, b + 1)
                nc.vector.scalar_tensor_tensor(out=kv_gate[p][:, :], in0=cols(q_tanh, b), scalar=1.0,
                                               in1=kv_sum[p][:, :], op0=ALU.add, op1=ALU.mult).then_inc(kv_gate_ok, 1)
                dve.wait_ge(kv_gate_ok, b + 1)
                dve.wait_ge(k_inv_ok, b + 1)
                nc.vector.tensor_tensor(o_t[p][:, :], kv_gate[p][:, :], k_inv[p][:, :],
                                        ALU.mult).then_inc(o_t_ok, 1)

            def mean_var(n, src, b):
                for t in range(NT):
                    st = nc.vector.bn_stats(stats[n][:, t, :], src[:, t, :])
                st.then_inc(stats_ok[n], 1)
                dve.wait_ge(stats_ok[n], b + 1)
                for t in range(NT):
                    ag = nc.vector.bn_aggr(mv[n][:, t, :], stats[n][:, t, :])
                ag.then_inc(mv_ok[n], 1)

            def ln1(b, p):
                dve.wait_ge(attn_in_ps, b + 1)
                if isinstance(b, int) and b == 0:
                    dve.wait_ge(in_x, 16)
                nc.vector.tensor_tensor(res1[p][:, :, :], attn_ps.rearrange("p (j d) -> p j d", d=D),
                                        x_tok[:, bass.ds(b * NT, NT), :], ALU.add).then_inc(res1_ok, 1)
                dve.wait_ge(res1_ok, b + 1)
                mean_var(0, res1[p], b)

            def choose(b, p):
                dve.wait_ge(logit_in_ps, b + 1)
                nc.vector.scalar_tensor_tensor(out=logits[p][:, :], in0=logit_ps, scalar=1.0 / S, in1=br_row,
                                               op0=ALU.mult, op1=ALU.add).then_inc(logits_ok, 1)
                dve.wait_ge(logits_ok, b + 1)
                nc.vector.max(top[p][:, :], logits[p][:, :]).then_inc(top_ok, 1)
                dve.wait_ge(top_ok, b + 1)
                nc.vector.max_index(top_i[p][:, :], top[p][:, :], logits[p][:, :]).then_inc(top_i_ok, 1)
                nc.vector.tensor_scalar(top_d[p][:, :], top[p][:, :], top[p][:, 0:1], None,
                                        ALU.subtract).then_inc(top_d_ok, 1)

            def soft_max(b, p):
                dve.wait_ge(th8_ok, b + 1)
                nc.vector.tensor_scalar(den8[p][:, :], th8[p][:, :], -1.0, 1.0, ALU.mult, ALU.add).then_inc(den8_ok, 1)
                dve.wait_ge(den8_ok, b + 1)
                nc.vector.reciprocal(inv8[p][:, :], den8[p][:, :]).then_inc(inv8_ok, 1)
                dve.wait_ge(inv8_ok, b + 1)
                nc.vector.tensor_scalar(exp8[p][:, :], inv8[p][:, :], 2.0, -1.0, ALU.mult, ALU.add).then_inc(exp8_ok, 1)
                dve.wait_ge(exp8_ok, b + 1)
                nc.vector.tensor_reduce(sum8[p][:, :], exp8[p][:, :], AX.X, ALU.add).then_inc(sum8_ok, 1)
                dve.wait_ge(sum8_ok, b + 1)
                nc.vector.reciprocal(isum8[p][:, :], sum8[p][:, :]).then_inc(isum8_ok, 1)
                dve.wait_ge(isum8_ok, b + 1)
                nc.vector.scalar_tensor_tensor(out=dp[p][:, :], in0=exp8[p][:, 0:1], scalar=exp8[p][:, 1:2],
                                               in1=isum8[p][:, :], op0=ALU.subtract, op1=ALU.mult).then_inc(dp_ok, 1)

            def weights(b, p):
                dve.wait_ge(th2_ok, b + 1)
                nc.vector.tensor_scalar(w_top[p][:, 0:1], th2[p][:, :], 0.5, 0.5, ALU.mult, ALU.add)
                nc.vector.tensor_scalar(w_top[p][:, 1:2], th2[p][:, :], -0.5, 0.5, ALU.mult,
                                        ALU.add).then_inc(w_top_ok, 1)

            def combine(b, p):
                v = out_ps[p][:, :].rearrange("p (k j d) -> p k j d", k=TOP_K, d=D)
                dve.wait_ge(x1_b2_ok, b + 1)
                dve.wait_ge(out_in_ps, 2 * b + 2)
                nc.vector.scalar_tensor_tensor(out=y0[:, :, :], in0=v[:, 0], scalar=w_top[p][:, 0:1],
                                               in1=x1_b2[p][:, :, :], op0=ALU.mult, op1=ALU.add).then_inc(y0_ok, 1)
                dve.wait_ge(y0_ok, b + 1)
                nc.vector.scalar_tensor_tensor(out=y[:, :, :], in0=v[:, 1], scalar=w_top[p][:, 1:2],
                                               in1=y0[:, :, :], op0=ALU.mult, op1=ALU.add).then_inc(y_ok, 1)
                dve.wait_ge(y_ok, b + 1)
                mean_var(1, y, b)

            def residual(b, p):
                dve.wait_ge(zg_ok, b + 1)
                nc.vector.tensor_tensor(u[:, :, :], zg[:, :, :], x1_beta[p][:, :, :], ALU.add).then_inc(u_ok, 1)
                dve.wait_ge(u_ok, b + 1)
                mean_var(2, u, b)

            dve.wait_ge(const_ok, 2)
            attn_denominator(0, 0)
            attn_numerator(0, 0)
            attn_denominator(1, 1)
            dve.wait_ge(in_small, 48)
            ln1(0, 0)
            attn_numerator(1, 1)
            ln1(1, 1)
            choose(0, 0)
            attn_denominator(2, 0)
            soft_max(0, 0)
            attn_numerator(2, 0)
            weights(0, 0)
            choose(1, 1)
            for b in range(B + 1):
                p = b % 2
                ahead = b + AHEAD < B
                if b + 1 < B:
                    soft_max(b + 1, 1 - p)
                if ahead:
                    ln1(b + AHEAD, p)
                if b > 0:
                    combine(b - 1, 1 - p)
                if b + AHEAD + 1 < B:
                    attn_denominator(b + AHEAD + 1, 1 - p)
                if b + 1 < B:
                    weights(b + 1, 1 - p)
                if b > 0:
                    residual(b - 1, 1 - p)
                if b + AHEAD + 1 < B:
                    attn_numerator(b + AHEAD + 1, 1 - p)
                if ahead:
                    choose(b + AHEAD, p)

        @block.gpsimd
        def _(pool):
            def rsqrt(n, b):
                pool.wait_ge(mv_ok[n], b + 1)
                nc.gpsimd.tensor_scalar(var_eps[n][:, :], mv[n][:, :, 1], LN_EPS, None, ALU.add).then_inc(eps_ok[n], 1)
                pool.wait_ge(eps_ok[n], b + 1)
                nc.gpsimd.tensor_tensor(rstd[n][:, :], var_eps[n][:, :], neg_half[:, :], ALU.pow).then_inc(rstd_ok[n], 1)
                pool.wait_ge(rstd_ok[n], b + 1)
                for t in range(NT):
                    s = nc.gpsimd.tensor_scalar(shift[n][:, t:t + 1], mv[n][:, t, 0:1], rstd[n][:, t:t + 1], -1.0,
                                                ALU.mult, ALU.mult)
                s.then_inc(shift_ok[n], 1)

            def bias_terms(b, p, i):
                pool.wait_ge(w_top_ok, b + 1)
                for k in range(TOP_K):
                    s = TOP_K * p + k
                    pool.wait_ge(b2_in[s], 16 * (i + 1))
                    m = nc.gpsimd.tensor_scalar(b2w[k][:, :], b2[s][:, :], w_top[p][:, k:k + 1], 1.0, ALU.mult,
                                                ALU.mult)
                m.then_inc(b2w_ok, 1)
                pool.wait_ge(b2w_ok, b + 1)
                nc.gpsimd.tensor_tensor(b2c[:, :], b2w[0][:, :], b2w[1][:, :], ALU.add).then_inc(b2c_ok, 1)
                pool.wait_ge(b2c_ok, b + 1)
                pool.wait_ge(x1_ok, b + 1)
                if not (isinstance(b, int) and b < 2):
                    pool.wait_ge(y0_ok, b - 1)
                    pool.wait_ge(u_ok, b - 1)
                nc.gpsimd.tensor_tensor(x1_b2[p][:, :, :], x1[p][:, :, :],
                                        b2c[:, :].unsqueeze(1).to_broadcast([128, NT, D]), ALU.add
                                        ).then_inc(x1_b2_ok, 1)
                nc.gpsimd.tensor_tensor(x1_beta[p][:, :, :], x1[p][:, :, :],
                                        beta_row.unsqueeze(1).to_broadcast([128, NT, D]), ALU.add
                                        ).then_inc(x1_beta_ok, 1)

            def scale_gamma(b):
                pool.wait_ge(z_ok, b + 1)
                nc.gpsimd.tensor_tensor(zg[:, :, :], z[:, :, :], gamma_row.unsqueeze(1).to_broadcast([128, NT, D]),
                                        ALU.mult).then_inc(zg_ok, 1)

            pool.wait_ge(const_ok, 2)
            rsqrt(0, 0)
            rsqrt(0, 1)
            pool.wait_ge(in_small, 48)
            bias_terms(0, 0, 0)
            for b in range(B + 1):
                p = b % 2
                ahead = b + AHEAD < B
                if ahead:
                    rsqrt(0, b + AHEAD)
                if b > 0:
                    rsqrt(1, b - 1)
                    scale_gamma(b - 1)
                    rsqrt(2, b - 1)
                if b + 1 < B:
                    bias_terms(b + 1, 1 - p, (b + 1) // 2)


_OUT = (8, 256, 128)


def kernel(**inputs):
    import numpy as _np
    import concourse.bacc as _bacc
    from concourse.bass_utils import run_bass_kernel_spmd as _run

    X = _np.asarray(inputs["L0_attn_X"])
    W1, W2 = _np.asarray(inputs["L0_ffn_W1"]), _np.asarray(inputs["L0_ffn_W2"])
    B, S, D = X.shape
    E, _, F = W1.shape
    NF = F // D
    row = lambda *names: [_np.asarray(inputs[n]).reshape(1, -1) for n in names]
    arrays = {
        "xt": X.transpose(2, 0, 1).reshape(D, B * S),
        "x": X,
        "wkvqc": _np.concatenate([_np.asarray(inputs["L0_attn_W" + n]) for n in "kvqc"], axis=1),
        "w1b": _np.concatenate([W1, _np.asarray(inputs["L0_ffn_b1"]).reshape(E, NF, D).transpose(0, 2, 1)], axis=2),
        "w2": W2.reshape(E, NF, D, D).transpose(0, 2, 1, 3).reshape(E, D, NF * D),
        "b2": _np.asarray(inputs["L0_ffn_b2"]),
        "wr": _np.asarray(inputs["L0_ffn_Wr"]),
        "rows": _np.concatenate(row("L0_ffn_br", "L0_ffn_gamma", "L0_ffn_beta"), axis=1),
        "ident": _np.eye(128, dtype=_np.float32),
    }
    arrays = {n: _np.ascontiguousarray(a) for n, a in arrays.items()}
    nc = _bacc.Bacc("TRN2", target_bir_lowering=False, num_devices=1)
    aps = [nc.dram_tensor("in_" + n, a.shape, F32, kind="ExternalInput").ap() for n, a in arrays.items()]
    out = nc.dram_tensor("out", X.shape, F32, kind="ExternalOutput").ap()
    attention_free_moe_block(nc, *aps, out)
    r = _run(nc, [{"in_" + n: a for n, a in arrays.items()}], core_ids=[0])
    return r.results[0]["out"]
```

```python
import concourse.bass as bass
from concourse import mybir
from contextlib import ExitStack

F32 = mybir.dt.float32
U32 = mybir.dt.uint32
ALU = mybir.AluOpType
ACT = mybir.ActivationFunctionType
AX = mybir.AxisListType

ATTN_EPS = 1e-6
LN_EPS = 1e-5
TOP_K = 2


def attention_free_moe_block(nc, xt_d, x_d, wkvqc_d, w1b_d, w2_d, b2_d, wr_d, rows_d, ident_d, out_d):
    B, S, D = x_d.shape
    E = w1b_d.shape[0]
    NF = w2_d.shape[2] // D
    F = NF * D
    NT = S // 128
    GB = 512 // S
    G, GS = B // GB, GB * S
    WARM = 3
    R = 4
    assert D == 128 and S == 256 and B % 2 == 0 and B >= 4

    with ExitStack() as ctx:
        def sb(name, shape, dt=F32):
            return ctx.enter_context(nc.sbuf_tensor(name, shape, dt))

        def psum(name, shape, dt=F32):
            return ctx.enter_context(nc.psum_tensor(name, shape, dt))

        def sem(name):
            return ctx.enter_context(nc.semaphore(name))

        xt = sb("xt", [D, B * S])
        x_tok = sb("x_tok", [128, B * NT, D])
        wkvqc = sb("wkvqc", [D, 4 * D])
        wc_half = sb("wc_half", [D, D])
        wr = sb("wr", [D, E])
        rows = sb("rows", [128, E + 2 * D])
        ident = sb("ident", [128, 128])
        ones = sb("ones", [128, S])
        gelu_warm = sb("gelu_warm", [128, 1])
        neg_half = sb("neg_half", [128, NT])
        br_row = rows[:, 0:E]
        gamma_row = rows[:, E:E + D]
        beta_row = rows[:, E + D:E + 2 * D]

        k_exp = sb("k_exp", [D, B * S])
        v_sb = sb("v_sb", [D, B * S])
        q_tanh = sb("q_tanh", [D, B * S])
        k_sum = [sb(f"k_sum{p}", [D, S]) for p in range(R)]
        k_inv = [sb(f"k_inv{p}", [D, S]) for p in range(R)]
        kv = [sb(f"kv{p}", [D, S]) for p in range(R)]
        kv_sum = [sb(f"kv_sum{p}", [D, S]) for p in range(R)]
        kv_gate = [sb(f"kv_gate{p}", [D, S]) for p in range(R)]
        o_t = [sb(f"o_t{p}", [D, S]) for p in range(R)]

        res1 = [sb(f"res1_{p}", [128, NT, D]) for p in range(R)]
        x1 = [sb(f"x1_{p}", [128, NT, D]) for p in range(R)]
        x1_t = [sb(f"x1_t{p}", [D, S]) for p in range(R)]
        x1_sum = [sb(f"x1_sum{p}", [D, 1]) for p in range(R)]
        logits = [sb(f"logits{p}", [128, E]) for p in range(R)]
        top = [sb(f"top{p}", [128, E]) for p in range(R)]
        top_i = [sb(f"top_i{p}", [128, E], U32) for p in range(R)]
        top_d = [sb(f"top_d{p}", [128, E]) for p in range(R)]
        th8 = [sb(f"th8_{p}", [128, E]) for p in range(R)]
        den8 = [sb(f"den8_{p}", [128, E]) for p in range(R)]
        inv8 = [sb(f"inv8_{p}", [128, E]) for p in range(R)]
        exp8 = [sb(f"exp8_{p}", [128, E]) for p in range(R)]
        sum8 = [sb(f"sum8_{p}", [128, 1]) for p in range(R)]
        isum8 = [sb(f"isum8_{p}", [128, 1]) for p in range(R)]
        dp = [sb(f"dp{p}", [128, 1]) for p in range(R)]
        th2 = [sb(f"th2_{p}", [128, 1]) for p in range(R)]
        w_top = [sb(f"w_top{p}", [128, TOP_K]) for p in range(R)]

        w1b = [sb(f"w1b{s}", [D, F + NF]) for s in range(R * TOP_K)]
        w2 = [sb(f"w2_{s}", [128, NF, D]) for s in range(R * TOP_K)]
        b2 = [sb(f"b2_{s}", [128, D]) for s in range(R * TOP_K)]
        h_t = [sb(f"h_t{k}", [128, NF, S]) for k in range(TOP_K)]
        b2w = [sb(f"b2w{k}", [128, D]) for k in range(TOP_K)]
        b2c = sb("b2c", [128, D])
        x1_b2 = [sb(f"x1_b2_{p}", [128, NT, D]) for p in range(R)]
        x1_beta = [sb(f"x1_beta{p}", [128, NT, D]) for p in range(R)]
        y0 = sb("y0", [128, NT, D])
        y = [sb(f"y_{p}", [128, NT, D]) for p in range(2)]
        z = sb("z", [128, NT, D])
        zg = sb("zg", [128, NT, D])
        u = [sb(f"u_{p}", [128, NT, D]) for p in range(2)]
        fin = [sb(f"fin{p}", [128, NT, D]) for p in range(2)]

        stats = [[sb(f"stats{n}_{p}", [128, NT, 6]) for p in range(R)] for n in range(3)]
        mv = [[sb(f"mv{n}_{p}", [128, NT, 2]) for p in range(R)] for n in range(3)]
        var_eps = [[sb(f"var_eps{n}_{p}", [128, NT]) for p in range(R)] for n in range(3)]
        neg_mean = [[sb(f"neg_mean{n}_{p}", [128, NT]) for p in range(R)] for n in range(3)]
        rstd = [[sb(f"rstd{n}_{p}", [128, NT]) for p in range(R)] for n in range(3)]
        shift = [[sb(f"shift{n}_{p}", [128, NT]) for p in range(R)] for n in range(3)]

        bank = [psum(f"bank{n}", [128, 512]) for n in range(8)]
        kvq_ps = [bank[0:3], bank[5:8]]
        attn_ps = bank[3][:, 0:S]
        x1t_ps = bank[4][:, 0:S]
        logit_ps = bank[4][:, S:S + E]
        h_ps = [bank[0:2], bank[5:7]]
        out_ps = [bank[2], bank[7]]

        in_k = sem("in_k")
        in_xt = [sem(f"in_xt{n}") for n in range(G)]
        in_x = sem("in_x")
        in_small = sem("in_small")
        const_ok = sem("const_ok")
        wc_ok = sem("wc_ok")
        k_in_ps = sem("k_in_ps")
        v_in_ps = sem("v_in_ps")
        q_in_ps = sem("q_in_ps")
        k_exp_ok = sem("k_exp_ok")
        v_ok = sem("v_ok")
        q_tanh_ok = sem("q_tanh_ok")
        k_sum_ok = sem("k_sum_ok")
        k_inv_ok = sem("k_inv_ok")
        kv_ok = sem("kv_ok")
        kv_sum_ok = sem("kv_sum_ok")
        kv_gate_ok = sem("kv_gate_ok")
        o_t_ok = sem("o_t_ok")
        attn_in_ps = sem("attn_in_ps")
        res1_ok = sem("res1_ok")
        stats_ok = [sem(f"stats_ok{n}") for n in range(3)]
        mv_ok = [sem(f"mv_ok{n}") for n in range(3)]
        neg_mean_ok = [sem(f"neg_mean_ok{n}") for n in range(3)]
        eps_ok = [sem(f"eps_ok{n}") for n in range(3)]
        rstd_ok = [sem(f"rstd_ok{n}") for n in range(3)]
        shift_ok = [sem(f"shift_ok{n}") for n in range(3)]
        x1_ok = sem("x1_ok")
        x1t_in_ps = sem("x1t_in_ps")
        x1_t_ok = sem("x1_t_ok")
        logit_in_ps = sem("logit_in_ps")
        logits_ok = sem("logits_ok")
        top_ok = sem("top_ok")
        top_i_ok = sem("top_i_ok")
        top_d_ok = sem("top_d_ok")
        th8_ok = sem("th8_ok")
        den8_ok = sem("den8_ok")
        inv8_ok = sem("inv8_ok")
        exp8_ok = sem("exp8_ok")
        sum8_ok = sem("sum8_ok")
        isum8_ok = sem("isum8_ok")
        dp_ok = sem("dp_ok")
        th2_ok = sem("th2_ok")
        w_top_ok = sem("w_top_ok")
        w1_in = [sem(f"w1_in{s}") for s in range(R * TOP_K)]
        w2_in = [sem(f"w2_in{s}") for s in range(R * TOP_K)]
        b2_in = [sem(f"b2_in{s}") for s in range(R * TOP_K)]
        h_in_ps = sem("h_in_ps")
        h_ok = sem("h_ok")
        out_in_ps = sem("out_in_ps")
        b2w_ok = sem("b2w_ok")
        b2c_ok = sem("b2c_ok")
        x1_b2_ok = sem("x1_b2_ok")
        x1_beta_ok = sem("x1_beta_ok")
        y0_ok = sem("y0_ok")
        y_ok = sem("y_ok")
        z_ok = sem("z_ok")
        zg_ok = sem("zg_ok")
        u_ok = sem("u_ok")
        center_ok = sem("center_ok")
        fin_last_ok = sem("fin_last_ok")
        fin_ok = sem("fin_ok")
        out_dma = [sem(f"out_dma{p}") for p in range(2)]

        block = ctx.enter_context(nc.Block())

        @block.sync
        def _(sp):
            for g in range(G):
                sp.dma_start(xt[:, g * GS:(g + 1) * GS], xt_d[:, g * GS:(g + 1) * GS]).then_inc(in_xt[g], 16)
                if g == 1:
                    sp.dma_start(wr[:, :], wr_d).then_inc(in_small, 16)
                    sp.dma_start(rows[:, :], rows_d.partition_broadcast(128)).then_inc(in_small, 16)
                    sp.dma_start(ident[:, :], ident_d).then_inc(in_small, 16)
                    sp.dma_start(x_tok[:, :, :], x_d.rearrange("b (j t) d -> t (b j) d", t=128)).then_inc(in_x, 16)

            def fetch(b):
                sp.wait_ge(top_i_ok, b + 1)
                if b >= R:
                    sp.wait_ge(out_in_ps, TOP_K * (b - R + 1))
                    sp.wait_ge(x1_b2_ok, b - R + 1)
                for k in range(TOP_K):
                    s = TOP_K * (b % R) + k
                    e = sp.value_load(top_i[b % R][0:1, k:k + 1], min_val=0, max_val=E - 1)
                    sp.dma_start(w1b[s][:, :], w1b_d[bass.ds(e, 1), :, :].rearrange("e p n -> (e p) n")
                                 ).then_inc(w1_in[s], 16)
                    sp.dma_start(w2[s][:, :, :].rearrange("p c d -> p (c d)"),
                                 w2_d[bass.ds(e, 1), :, :].rearrange("e p n -> (e p) n")).then_inc(w2_in[s], 16)
                    sp.dma_start(b2[s][:, :], b2_d[bass.ds(e, 1), :].partition_broadcast(128)
                                 .rearrange("p e d -> p (e d)")).then_inc(b2_in[s], 16)

            def store(b):
                sp.wait_ge(fin_ok, b + 1)
                sp.dma_start(out_d[b, :, :].rearrange("(j t) d -> t j d", t=128),
                             fin[b % 2][:, :, :]).then_inc(out_dma[b % 2], 16)

            for b in range(B):
                fetch(b)
                if b >= 3:
                    store(b - 3)
            for b in range(B - 3, B):
                if b == B - 1:
                    sp.wait_ge(fin_last_ok, 1)
                store(b)
            for p in range(2):
                sp.wait_ge(out_dma[p], 16 * (B // 2))

        @block.tensor
        def _(pe):
            def project(g, n, ready, read):
                pe.wait_ge(in_xt[g], 16)
                if g >= 2:
                    pe.wait_ge(read, g - 1)
                pe.matmul(kvq_ps[g % 2][n][:, :], wkvqc[:, n * D:(n + 1) * D], xt[:, g * GS:(g + 1) * GS],
                          start=True, stop=True).then_inc(ready, 1)

            def project_k(g):
                project(g, 0, k_in_ps, k_exp_ok)

            def project_v(g):
                project(g, 1, v_in_ps, v_ok)

            def project_q(g):
                project(g, 2, q_in_ps, q_tanh_ok)

            def attn_out(b):
                pe.wait_ge(o_t_ok, b + 1)
                if b == 0:
                    pe.wait_ge(wc_ok, 1)
                else:
                    pe.wait_ge(res1_ok, b)
                for t in range(NT):
                    mm = pe.matmul(attn_ps[:, t * D:(t + 1) * D], o_t[b % R][:, t * 128:(t + 1) * 128], wc_half[:, :],
                                   start=True, stop=True)
                mm.then_inc(attn_in_ps, 1)

            def transpose_x1(b):
                pe.wait_ge(x1_ok, b + 1)
                if b == 0:
                    pe.wait_ge(in_small, 48)
                else:
                    pe.wait_ge(logits_ok, b)
                for t in range(NT):
                    mm = pe.transpose(x1t_ps[:, t * 128:(t + 1) * 128], x1[b % R][:, t, :], ident[:, :])
                mm.then_inc(x1t_in_ps, 1)

            def router(b):
                pe.wait_ge(x1_t_ok, b + 1)
                pe.matmul(logit_ps, x1_sum[b % R][:, 0:1].to_broadcast([D, 128]), wr[:, :], start=True,
                          stop=True).then_inc(logit_in_ps, 1)

            def up(b, k):
                s = TOP_K * (b % R) + k
                pe.wait_ge(w1_in[s], 16 * (b // R + 1))
                if b == 0:
                    pe.wait_ge(v_ok, G - 1 + k)
                else:
                    pe.wait_ge(h_ok, TOP_K * (b - 1) + k + 1)
                for c in range(NF):
                    mm = pe.matmul(h_ps[k][c // 2][:, (c % 2) * S:(c % 2 + 1) * S], w1b[s][:, c * D:(c + 1) * D],
                                   x1_t[b % R][:, :], start=True, stop=True)
                    if c % 2:
                        mm.then_inc(h_in_ps, 1)

            def down(b, k):
                s = TOP_K * (b % R) + k
                pe.wait_ge(w2_in[s], 16 * (b // R + 1))
                pe.wait_ge(h_ok, TOP_K * b + k + 1)
                if k == 0 and b < 2:
                    pe.wait_ge(q_tanh_ok, G - 1 + b)
                if k == 0 and b >= 2:
                    pe.wait_ge(y_ok, b - 1)
                for t in range(NT):
                    for c in range(NF):
                        mm = pe.matmul(out_ps[b % 2][:, k * S + t * D:k * S + (t + 1) * D],
                                       h_t[k][:, c, t * 128:(t + 1) * 128], w2[s][:, c, :],
                                       start=(c == 0), stop=(c == NF - 1))
                mm.then_inc(out_in_ps, 1)

            pe.wait_ge(const_ok, 1)
            for n in range(WARM):
                pe.matmul(bank[4][:, 0:S], ones[:, 0:128], ones[:, :], start=True, stop=True)
            pe.wait_ge(in_k, 16)
            for g in range(2):
                project_k(g)
                project_v(g)
                project_q(g)
            attn_out(0)
            project_k(2)
            project_v(2)
            project_q(2)
            project_k(3)
            project_v(3)
            attn_out(1)
            transpose_x1(0)
            router(0)
            project_q(3)
            attn_out(2)
            transpose_x1(1)
            router(1)
            up(0, 0)
            for b in range(B):
                if 0 < b and b + 2 < B:
                    transpose_x1(b + 2)
                up(b, 1)
                if b == 0:
                    transpose_x1(b + 2)
                if b + 3 < B:
                    attn_out(b + 3)
                down(b, 0)
                if b + 2 < B:
                    router(b + 2)
                if b + 1 < B:
                    up(b + 1, 0)
                down(b, 1)

        @block.scalar
        def _(act):
            act.dma_start(wkvqc[:, :], wkvqc_d).then_inc(in_k, 16)

            def columns(g):
                return slice(g * GS, (g + 1) * GS)

            def exp_k(g):
                act.wait_ge(k_in_ps, g + 1)
                nc.scalar.activation(k_exp[:, columns(g)], kvq_ps[g % 2][0][:, :], ACT.Exp).then_inc(k_exp_ok, 1)

            def copy_v(g):
                act.wait_ge(v_in_ps, g + 1)
                nc.scalar.copy(v_sb[:, columns(g)], kvq_ps[g % 2][1][:, :]).then_inc(v_ok, 1)

            def tanh_q(g):
                act.wait_ge(q_in_ps, g + 1)
                nc.scalar.activation(q_tanh[:, columns(g)], kvq_ps[g % 2][2][:, :], ACT.Tanh,
                                     scale=0.5).then_inc(q_tanh_ok, 1)

            def norm(n, src, dst, b, done, tiles=NT):
                act.wait_ge(shift_ok[n], b + 1)
                for t in range(tiles):
                    a = nc.scalar.activation(dst[:, t, :], src[:, t, :], ACT.Identity, bias=shift[n][b % R][:, t:t + 1],
                                             scale=rstd[n][b % R][:, t:t + 1])
                a.then_inc(done, 1)

            def norm1(b):
                if b >= R:
                    act.wait_ge(x1_beta_ok, b - R + 1)
                norm(0, res1[b % R], x1[b % R], b, x1_ok)

            def evacuate_x1t(b):
                act.wait_ge(x1t_in_ps, b + 1)
                nc.scalar.activation(x1_t[b % R][:, :], x1t_ps, ACT.Identity,
                                     accum_out=x1_sum[b % R][:, :]).then_inc(x1_t_ok, 1)

            def gelu(b, k):
                q = TOP_K * b + k
                if b >= 1:
                    act.wait_ge(out_in_ps, q - 1)
                for c in range(NF):
                    if c % 2 == 0:
                        act.wait_ge(h_in_ps, NF // 2 * q + c // 2 + 1)
                    a = nc.scalar.activation(h_t[k][:, c, :], h_ps[k][c // 2][:, (c % 2) * S:(c % 2 + 1) * S],
                                             ACT.Gelu, bias=w1b[TOP_K * (b % R) + k][:, F + c:F + c + 1])
                a.then_inc(h_ok, 1)

            def router_tanh8(b):
                act.wait_ge(top_d_ok, b + 1)
                nc.scalar.activation(th8[b % R][:, :], top_d[b % R][:, :], ACT.Tanh, scale=0.5).then_inc(th8_ok, 1)

            def router_tanh2(b):
                act.wait_ge(dp_ok, b + 1)
                nc.scalar.activation(th2[b % R][:, :], dp[b % R][:, :], ACT.Tanh, scale=0.5).then_inc(th2_ok, 1)

            def norm2(b):
                norm(1, y[b % 2], z, b, z_ok)

            def norm3(b):
                if b >= 2:
                    act.wait_ge(out_dma[b % 2], 16 * (b // 2))
                norm(2, u[b % 2], fin[b % 2], b, fin_ok, NT if b < B - 1 else 1)

            for g in range(3):
                exp_k(g)
                copy_v(g)
                tanh_q(g)
            norm1(0)
            exp_k(3)
            copy_v(3)
            evacuate_x1t(0)
            tanh_q(3)
            act.wait_ge(const_ok, 2)
            nc.scalar.activation(gelu_warm[:, :], ones[:, 0:1], ACT.Gelu)
            norm1(1)
            evacuate_x1t(1)
            router_tanh8(0)
            norm1(2)
            gelu(0, 0)
            router_tanh8(1)
            for b in range(B + 1):
                if 0 < b and b + 2 < B:
                    evacuate_x1t(b + 2)
                if b < B:
                    gelu(b, 1)
                if b > 1:
                    norm3(b - 2)
                if b == 0:
                    evacuate_x1t(b + 2)
                if b < B:
                    router_tanh2(b)
                if 0 < b < B:
                    norm2(b - 1)
                if b + 3 < B:
                    norm1(b + 3)
                if b + 1 < B:
                    gelu(b + 1, 0)
                if b + 2 < B:
                    router_tanh8(b + 2)
            norm3(B - 1)

        @block.vector
        def _(dve):
            def cols(a, b):
                return a[:, b * S:(b + 1) * S]

            def sum_keys(b):
                dve.wait_ge(k_exp_ok, b // GB + 1)
                nc.vector.tensor_tensor_scan(k_sum[b % R][:, :], ones[:, :], cols(k_exp, b), ATTN_EPS, ALU.mult,
                                             ALU.add).then_inc(k_sum_ok, 1)

            def invert_keys(b):
                dve.wait_ge(k_sum_ok, b + 1)
                nc.vector.reciprocal(k_inv[b % R][:, :], k_sum[b % R][:, :]).then_inc(k_inv_ok, 1)

            def sum_kv(b):
                dve.wait_ge(kv_ok, b + 1)
                nc.vector.tensor_tensor_scan(kv_sum[b % R][:, :], ones[:, :], kv[b % R][:, :], 0.0, ALU.mult,
                                             ALU.add).then_inc(kv_sum_ok, 1)

            def gate_kv(b):
                dve.wait_ge(q_tanh_ok, b // GB + 1)
                dve.wait_ge(kv_sum_ok, b + 1)
                nc.vector.scalar_tensor_tensor(out=kv_gate[b % R][:, :], in0=cols(q_tanh, b), scalar=1.0,
                                               in1=kv_sum[b % R][:, :], op0=ALU.add,
                                               op1=ALU.mult).then_inc(kv_gate_ok, 1)

            def attend(b):
                dve.wait_ge(kv_gate_ok, b + 1)
                dve.wait_ge(k_inv_ok, b + 1)
                nc.vector.tensor_tensor(o_t[b % R][:, :], kv_gate[b % R][:, :], k_inv[b % R][:, :],
                                        ALU.mult).then_inc(o_t_ok, 1)

            def add_x(b):
                dve.wait_ge(attn_in_ps, b + 1)
                nc.vector.tensor_tensor(res1[b % R][:, :, :], attn_ps.rearrange("p (j d) -> p j d", d=D),
                                        x_tok[:, b * NT:(b + 1) * NT, :], ALU.add).then_inc(res1_ok, 1)

            def tile_stats(n, src, b, ready):
                dve.wait_ge(ready, b + 1)
                for t in range(NT):
                    nc.vector.bn_stats(stats[n][b % R][:, t, :], src[:, t, :]).then_inc(stats_ok[n], 1)
                for t in range(NT):
                    dve.wait_ge(stats_ok[n], NT * b + t + 1)
                    nc.vector.bn_aggr(mv[n][b % R][:, t, :], stats[n][b % R][:, t, :]).then_inc(mv_ok[n], 1)

            def prepare_norm(n, b):
                dve.wait_ge(mv_ok[n], NT * (b + 1))
                nc.vector.tensor_scalar(var_eps[n][b % R][:, :], mv[n][b % R][:, :, 1], LN_EPS, None, ALU.add).then_inc(eps_ok[n], 1)
                nc.vector.tensor_scalar(neg_mean[n][b % R][:, :], mv[n][b % R][:, :, 0], -1.0, None,
                                        ALU.mult).then_inc(neg_mean_ok[n], 1)

            def add_br(b):
                dve.wait_ge(logit_in_ps, b + 1)
                nc.vector.scalar_tensor_tensor(out=logits[b % R][:, :], in0=logit_ps, scalar=1.0 / S, in1=br_row,
                                               op0=ALU.mult, op1=ALU.add).then_inc(logits_ok, 1)

            def sort_logits(b):
                dve.wait_ge(logits_ok, b + 1)
                nc.vector.max(top[b % R][:, :], logits[b % R][:, :]).then_inc(top_ok, 1)

            def find_experts(b):
                dve.wait_ge(top_ok, b + 1)
                nc.vector.max_index(top_i[b % R][:, :], top[b % R][:, :], logits[b % R][:, :]).then_inc(top_i_ok, 1)

            def below_top(b):
                nc.vector.tensor_scalar(top_d[b % R][:, :], top[b % R][:, :], top[b % R][:, 0:1], None,
                                        ALU.subtract).then_inc(top_d_ok, 1)

            def exp_denominator(b):
                dve.wait_ge(th8_ok, b + 1)
                nc.vector.tensor_scalar(den8[b % R][:, :], th8[b % R][:, :], -1.0, 1.0, ALU.mult,
                                        ALU.add).then_inc(den8_ok, 1)

            def exp_inverse(b):
                dve.wait_ge(den8_ok, b + 1)
                nc.vector.reciprocal(inv8[b % R][:, :], den8[b % R][:, :]).then_inc(inv8_ok, 1)

            def exp_value(b):
                dve.wait_ge(inv8_ok, b + 1)
                nc.vector.tensor_scalar(exp8[b % R][:, :], inv8[b % R][:, :], 2.0, -1.0, ALU.mult,
                                        ALU.add).then_inc(exp8_ok, 1)

            def exp_sum(b):
                dve.wait_ge(exp8_ok, b + 1)
                nc.vector.tensor_reduce(sum8[b % R][:, :], exp8[b % R][:, :], AX.X, ALU.add).then_inc(sum8_ok, 1)

            def exp_sum_inverse(b):
                dve.wait_ge(sum8_ok, b + 1)
                nc.vector.reciprocal(isum8[b % R][:, :], sum8[b % R][:, :]).then_inc(isum8_ok, 1)

            def top_two_apart(b):
                dve.wait_ge(isum8_ok, b + 1)
                nc.vector.scalar_tensor_tensor(out=dp[b % R][:, :], in0=exp8[b % R][:, 0:1],
                                               scalar=exp8[b % R][:, 1:2], in1=isum8[b % R][:, :],
                                               op0=ALU.subtract, op1=ALU.mult).then_inc(dp_ok, 1)

            def top_weights(b):
                dve.wait_ge(th2_ok, b + 1)
                nc.vector.tensor_scalar(w_top[b % R][:, 0:1], th2[b % R][:, :], 0.5, 0.5, ALU.mult, ALU.add)
                nc.vector.tensor_scalar(w_top[b % R][:, 1:2], th2[b % R][:, :], -0.5, 0.5, ALU.mult,
                                        ALU.add).then_inc(w_top_ok, 1)

            def combine_first(b):
                dve.wait_ge(x1_b2_ok, b + 1)
                dve.wait_ge(out_in_ps, TOP_K * (b + 1))
                nc.vector.scalar_tensor_tensor(out=y0[:, :, :], in0=expert_out(b, 0), scalar=w_top[b % R][:, 0:1],
                                               in1=x1_b2[b % R][:, :, :], op0=ALU.mult,
                                               op1=ALU.add).then_inc(y0_ok, 1)

            def combine_second(b):
                dve.wait_ge(y0_ok, b + 1)
                nc.vector.scalar_tensor_tensor(out=y[b % 2][:, :, :], in0=expert_out(b, 1),
                                               scalar=w_top[b % R][:, 1:2], in1=y0[:, :, :], op0=ALU.mult,
                                               op1=ALU.add).then_inc(y_ok, 1)

            def expert_out(b, k):
                return out_ps[b % 2][:, k * S:(k + 1) * S].rearrange("p (j d) -> p j d", d=D)

            def add_x1(b):
                dve.wait_ge(zg_ok, b + 1)
                nc.vector.tensor_tensor(u[b % 2][:, :, :], zg[:, :, :], x1_beta[b % R][:, :, :],
                                        ALU.add).then_inc(u_ok, 1)

            def center_last(b):
                dve.wait_ge(neg_mean_ok[1], b + 1)
                for t in range(NT):
                    c = nc.vector.scalar_tensor_tensor(out=z[:, t, :], in0=y[b % 2][:, t, :],
                                                       scalar=neg_mean[1][b % R][:, t:t + 1], in1=gamma_row,
                                                       op0=ALU.add, op1=ALU.mult)
                c.then_inc(center_ok, 1)

            def scale_last(b):
                dve.wait_ge(center_ok, 1)
                dve.wait_ge(rstd_ok[1], b + 1)
                for t in range(NT):
                    c = nc.vector.scalar_tensor_tensor(out=u[b % 2][:, t, :], in0=z[:, t, :],
                                                       scalar=rstd[1][b % R][:, t:t + 1],
                                                       in1=x1_beta[b % R][:, t, :], op0=ALU.mult, op1=ALU.add)
                c.then_inc(u_ok, 1)

            def finish_last(b):
                dve.wait_ge(shift_ok[2], b + 1)
                dve.wait_ge(out_dma[b % 2], 16 * (b // 2))
                for t in range(1, NT):
                    c = nc.vector.tensor_scalar(fin[b % 2][:, t, :], u[b % 2][:, t, :], rstd[2][b % R][:, t:t + 1],
                                                shift[2][b % R][:, t:t + 1], ALU.mult, ALU.add)
                c.then_inc(fin_last_ok, 1)

            nc.vector.memset(ones[:, :], 1.0).then_inc(const_ok, 1)
            nc.vector.memset(neg_half[:, :], -0.5).then_inc(const_ok, 1)
            dve.wait_ge(in_k, 16)
            nc.vector.tensor_scalar(wc_half[:, :], wkvqc[:, 3 * D:4 * D], 0.5, None, ALU.mult).then_inc(wc_ok, 1)
            dve.wait_ge(const_ok, 2)
            sum_keys(0)
            invert_keys(0)
            sum_kv(0)
            gate_kv(0)
            sum_keys(1)
            attend(0)
            sum_kv(1)
            sum_keys(2)
            dve.wait_ge(in_x, 16)
            add_x(0)
            tile_stats(0, res1[0], 0, res1_ok)
            gate_kv(1)
            prepare_norm(0, 0)
            invert_keys(1)
            attend(1)
            sum_keys(3)
            sum_kv(2)
            add_x(1)
            tile_stats(0, res1[1], 1, res1_ok)
            gate_kv(2)
            prepare_norm(0, 1)
            dve.wait_ge(in_small, 48)
            add_br(0)
            sort_logits(0)
            find_experts(0)
            invert_keys(2)
            below_top(0)
            attend(2)
            sum_kv(3)
            add_x(2)
            tile_stats(0, res1[2], 2, res1_ok)
            gate_kv(3)
            prepare_norm(0, 2)
            exp_denominator(0)
            add_br(1)
            exp_inverse(0)
            sort_logits(1)
            exp_value(0)
            find_experts(1)
            below_top(1)
            exp_sum(0)
            invert_keys(3)
            attend(3)
            for b in range(B + 1):
                last, now, soon, attn, far = b - 1, b, b + 2, b + 3, b + 4
                if b > 0:
                    combine_first(last)
                if now < B:
                    exp_sum_inverse(now)
                if b > 0:
                    combine_second(last)
                if now < B:
                    top_two_apart(now)
                if b > 0:
                    tile_stats(1, y[last % 2], last, y_ok)
                if far < B:
                    sum_keys(far)
                if b > 0:
                    prepare_norm(1, last)
                if far < B:
                    invert_keys(far)
                if attn < B:
                    add_x(attn)
                if attn < B:
                    tile_stats(0, res1[attn % R], attn, res1_ok)
                if now < B:
                    top_weights(now)
                if attn < B:
                    prepare_norm(0, attn)
                if soon < B:
                    add_br(soon)
                if far < B:
                    sum_kv(far)
                if soon < B:
                    sort_logits(soon)
                if b + 1 < B:
                    exp_denominator(b + 1)
                if soon < B:
                    find_experts(soon)
                    below_top(soon)
                if 0 < b < B:
                    add_x1(last)
                if b == B:
                    center_last(last)
                    scale_last(last)
                if b + 1 < B:
                    exp_inverse(b + 1)
                if far < B:
                    gate_kv(far)
                if b > 0:
                    tile_stats(2, u[last % 2], last, u_ok)
                if b + 1 < B:
                    exp_value(b + 1)
                if far < B:
                    attend(far)
                if b > 0:
                    prepare_norm(2, last)
                if b + 1 < B:
                    exp_sum(b + 1)
            finish_last(B - 1)

        @block.gpsimd
        def _(pool):
            def k_times_v(b):
                pool.wait_ge(k_exp_ok, b // GB + 1)
                pool.wait_ge(v_ok, b // GB + 1)
                if b >= R:
                    pool.wait_ge(kv_sum_ok, b - R + 1)
                nc.gpsimd.tensor_tensor(kv[b % R][:, :], k_exp[:, b * S:(b + 1) * S], v_sb[:, b * S:(b + 1) * S],
                                        ALU.mult).then_inc(kv_ok, 1)

            def rsqrt(n, b):
                pool.wait_ge(eps_ok[n], b + 1)
                nc.gpsimd.tensor_tensor(rstd[n][b % R][:, :], var_eps[n][b % R][:, :], neg_half[:, :], ALU.pow).then_inc(rstd_ok[n], 1)
                pool.wait_ge(neg_mean_ok[n], b + 1)
                pool.wait_ge(rstd_ok[n], b + 1)
                nc.gpsimd.tensor_tensor(shift[n][b % R][:, :], neg_mean[n][b % R][:, :], rstd[n][b % R][:, :],
                                        ALU.mult).then_inc(shift_ok[n], 1)

            def weigh_b2(b):
                pool.wait_ge(w_top_ok, b + 1)
                for k in range(TOP_K):
                    s = TOP_K * (b % R) + k
                    pool.wait_ge(b2_in[s], 16 * (b // R + 1))
                    m = nc.gpsimd.tensor_scalar(b2w[k][:, :], b2[s][:, :], w_top[b % R][:, k:k + 1], 1.0, ALU.mult,
                                                ALU.mult)
                m.then_inc(b2w_ok, 1)
                pool.wait_ge(b2w_ok, b + 1)
                nc.gpsimd.tensor_tensor(b2c[:, :], b2w[0][:, :], b2w[1][:, :], ALU.add).then_inc(b2c_ok, 1)

            def add_b2(b):
                pool.wait_ge(b2c_ok, b + 1)
                pool.wait_ge(x1_ok, b + 1)
                nc.gpsimd.tensor_tensor(x1_b2[b % R][:, :, :], x1[b % R][:, :, :],
                                        b2c[:, :].unsqueeze(1).to_broadcast([128, NT, D]), ALU.add
                                        ).then_inc(x1_b2_ok, 1)

            def add_beta(b):
                pool.wait_ge(x1_ok, b + 1)
                nc.gpsimd.tensor_tensor(x1_beta[b % R][:, :, :], x1[b % R][:, :, :],
                                        beta_row.unsqueeze(1).to_broadcast([128, NT, D]), ALU.add
                                        ).then_inc(x1_beta_ok, 1)

            def scale_gamma(b):
                pool.wait_ge(z_ok, b + 1)
                nc.gpsimd.tensor_tensor(zg[:, :, :], z[:, :, :], gamma_row.unsqueeze(1).to_broadcast([128, NT, D]),
                                        ALU.mult).then_inc(zg_ok, 1)

            k_times_v(0)
            k_times_v(1)
            pool.wait_ge(const_ok, 2)
            rsqrt(0, 0)
            k_times_v(2)
            rsqrt(0, 1)
            k_times_v(3)
            pool.wait_ge(in_small, 48)
            rsqrt(0, 2)
            for b in range(B + 1):
                if b + 4 < B:
                    k_times_v(b + 4)
                if b > 0:
                    rsqrt(1, b - 1)
                if b < B:
                    add_beta(b)
                if 0 < b < B:
                    scale_gamma(b - 1)
                if b + 3 < B:
                    rsqrt(0, b + 3)
                if b < B:
                    weigh_b2(b)
                    add_b2(b)
                if b > 0:
                    rsqrt(2, b - 1)


def kernel(**inputs):
    import numpy as _np
    import concourse.bacc as _bacc
    from concourse.bass_utils import run_bass_kernel_spmd as _run

    X = _np.asarray(inputs["L0_attn_X"])
    W1, W2 = _np.asarray(inputs["L0_ffn_W1"]), _np.asarray(inputs["L0_ffn_W2"])
    B, S, D = X.shape
    E, _, F = W1.shape
    NF = F // D
    row = lambda *names: [_np.asarray(inputs[n]).reshape(1, -1) for n in names]
    arrays = {
        "xt": X.transpose(2, 0, 1).reshape(D, B * S),
        "x": X,
        "wkvqc": _np.concatenate([_np.asarray(inputs["L0_attn_W" + n]) for n in "kvqc"], axis=1),
        "w1b": _np.concatenate([W1, _np.asarray(inputs["L0_ffn_b1"]).reshape(E, NF, D).transpose(0, 2, 1)], axis=2),
        "w2": W2.reshape(E, NF, D, D).transpose(0, 2, 1, 3).reshape(E, D, NF * D),
        "b2": _np.asarray(inputs["L0_ffn_b2"]),
        "wr": _np.asarray(inputs["L0_ffn_Wr"]),
        "rows": _np.concatenate(row("L0_ffn_br", "L0_ffn_gamma", "L0_ffn_beta"), axis=1),
        "ident": _np.eye(128, dtype=_np.float32),
    }
    arrays = {n: _np.ascontiguousarray(a) for n, a in arrays.items()}
    nc = _bacc.Bacc("TRN2", target_bir_lowering=False, num_devices=1)
    aps = [nc.dram_tensor("in_" + n, a.shape, F32, kind="ExternalInput").ap() for n, a in arrays.items()]
    out = nc.dram_tensor("out", X.shape, F32, kind="ExternalOutput").ap()
    attention_free_moe_block(nc, *aps, out)
    r = _run(nc, [{"in_" + n: a for n, a in arrays.items()}], core_ids=[0])
    return r.results[0]["out"]
```

```python
import concourse.bass as bass
from concourse import mybir
from contextlib import ExitStack

F32 = mybir.dt.float32
U32 = mybir.dt.uint32
ALU = mybir.AluOpType
ACT = mybir.ActivationFunctionType
AX = mybir.AxisListType

ATTN_EPS = 1e-6
LN_EPS = 1e-5
TOP_K = 2


def attention_free_moe_block(nc, xt_d, x_d, wkvqc_d, w1b_d, w2_d, b2_d, wr_d, rows_d, ident_d, out_d):
    B, S, D = x_d.shape
    E = w1b_d.shape[0]
    NF = w2_d.shape[2] // D
    F = NF * D
    NT = S // 128
    GB = 512 // S
    G, GS = B // GB, GB * S
    P = G + GB - 1
    WARM = 3
    R = 4
    assert D == 128 and S == 256 and B % 2 == 0 and B >= 6

    DVE_NORM2 = B - 2
    with ExitStack() as ctx:
        def sb(name, shape, dt=F32):
            return ctx.enter_context(nc.sbuf_tensor(name, shape, dt))

        def psum(name, shape, dt=F32):
            return ctx.enter_context(nc.psum_tensor(name, shape, dt))

        def sem(name):
            return ctx.enter_context(nc.semaphore(name))

        xt = sb("xt", [D, B * S])
        x_tok = sb("x_tok", [128, B * NT, D])
        wkvqc = sb("wkvqc", [D, 4 * D])
        wc_half = sb("wc_half", [D, D])
        wr = sb("wr", [D, E])
        rows = sb("rows", [128, E + 2 * D])
        ident = sb("ident", [128, 128])
        ones = sb("ones", [128, S])
        gelu_warm = sb("gelu_warm", [128, 1])
        sqrt_warm = sb("sqrt_warm", [128, 1])
        eps_col = sb("eps_col", [128, 1])
        neg_half = sb("neg_half", [128, NT])
        br_row = rows[:, 0:E]
        gamma_row = rows[:, E:E + D]
        beta_row = rows[:, E + D:E + 2 * D]

        k_exp = sb("k_exp", [D, B * S])
        v_sb = sb("v_sb", [D, B * S])
        q_tanh = sb("q_tanh", [D, B * S])
        k_sum = [sb(f"k_sum{p}", [D, S]) for p in range(R)]
        k_inv = [sb(f"k_inv{p}", [D, S]) for p in range(R)]
        kv = [sb(f"kv{p}", [D, S]) for p in range(R)]
        kv_sum = [sb(f"kv_sum{p}", [D, S]) for p in range(R)]
        kv_gate = [sb(f"kv_gate{p}", [D, S]) for p in range(R)]
        o_t = [sb(f"o_t{p}", [D, S]) for p in range(R)]

        res1 = [sb(f"res1_{p}", [128, NT, D]) for p in range(R)]
        x1 = [sb(f"x1_{p}", [128, NT, D]) for p in range(R)]
        x1_t = [sb(f"x1_t{p}", [D, S]) for p in range(R)]
        x1_sum = [sb(f"x1_sum{p}", [D, 1]) for p in range(R)]
        logits = [sb(f"logits{p}", [128, E]) for p in range(R)]
        top = [sb(f"top{p}", [128, E]) for p in range(R)]
        top_i = [sb(f"top_i{p}", [128, E], U32) for p in range(R)]
        top_d = [sb(f"top_d{p}", [128, E]) for p in range(R)]
        th8 = [sb(f"th8_{p}", [128, E]) for p in range(R)]
        den8 = [sb(f"den8_{p}", [128, E]) for p in range(R)]
        inv8 = [sb(f"inv8_{p}", [128, E]) for p in range(R)]
        exp8 = [sb(f"exp8_{p}", [128, E]) for p in range(R)]
        sum8 = [sb(f"sum8_{p}", [128, 1]) for p in range(R)]
        isum8 = [sb(f"isum8_{p}", [128, 1]) for p in range(R)]
        dp = [sb(f"dp{p}", [128, 1]) for p in range(R)]
        th2 = [sb(f"th2_{p}", [128, 1]) for p in range(R)]
        w_top = [sb(f"w_top{p}", [128, TOP_K]) for p in range(R)]

        w1b = [sb(f"w1b{s}", [D, F + NF]) for s in range(R * TOP_K)]
        w2 = [sb(f"w2_{s}", [128, NF, D]) for s in range(R * TOP_K)]
        b2 = [sb(f"b2_{s}", [128, D]) for s in range(R * TOP_K)]
        h_t = [sb(f"h_t{k}", [128, NF, S]) for k in range(TOP_K)]
        b2w = [sb(f"b2w{k}", [128, D]) for k in range(TOP_K)]
        b2c = sb("b2c", [128, D])
        x1_b2 = [sb(f"x1_b2_{p}", [128, NT, D]) for p in range(R)]
        x1_beta = [sb(f"x1_beta{p}", [128, NT, D]) for p in range(R)]
        y0 = sb("y0", [128, NT, D])
        y = [sb(f"y_{p}", [128, NT, D]) for p in range(2)]
        z = sb("z", [128, NT, D])
        zg = sb("zg", [128, NT, D])
        u = [sb(f"u_{p}", [128, NT, D]) for p in range(2)]
        fin = [sb(f"fin{p}", [128, NT, D]) for p in range(2)]

        stats = [[sb(f"stats{n}_{p}", [128, NT, 6]) for p in range(R)] for n in range(3)]
        mv = [[sb(f"mv{n}_{p}", [128, NT, 2]) for p in range(R)] for n in range(3)]
        var_eps = [[sb(f"var_eps{n}_{p}", [128, NT]) for p in range(R)] for n in range(3)]
        neg_mean = [[sb(f"neg_mean{n}_{p}", [128, NT]) for p in range(R)] for n in range(3)]
        rstd = [[sb(f"rstd{n}_{p}", [128, NT]) for p in range(R)] for n in range(3)]
        shift = [[sb(f"shift{n}_{p}", [128, NT]) for p in range(R)] for n in range(3)]
        std = [sb(f"std{n}", [128, NT]) for n in range(3)]
        last_rstd = [sb(f"last_rstd{n}", [128, NT]) for n in range(3)]

        bank = [psum(f"bank{n}", [128, 512]) for n in range(8)]
        kvq_ps = [bank[0:3], bank[5:8]]
        first_kvq_ps = [[bank[3][:, 0:S], bank[4][:, 0:S], bank[2][:, 0:S]],
                        [bank[0][:, 0:S], bank[1][:, 0:S], bank[2][:, S:2 * S]]]
        warm_ps = bank[2][:, 0:S]
        attn_ps = bank[3][:, 0:S]
        x1t_ps = bank[4][:, 0:S]
        logit_ps = bank[4][:, S:S + E]
        h_ps = [bank[0:2], bank[5:7]]
        out_ps = [bank[2], bank[7]]
        last_out_ps = [out_ps[0][:, 0:D], h_ps[0][0][:, 0:D]]

        in_k = sem("in_k")
        in_vqc = sem("in_vqc")
        in_xt = [sem(f"in_xt{n}") for n in range(P)]
        in_x = [sem(f"in_x{n}") for n in range(2)]
        in_small = sem("in_small")
        const_ok = sem("const_ok")
        wc_ok = sem("wc_ok")
        k_in_ps = sem("k_in_ps")
        v_in_ps = sem("v_in_ps")
        q_in_ps = sem("q_in_ps")
        k_exp_ok = sem("k_exp_ok")
        v_ok = sem("v_ok")
        q_tanh_ok = sem("q_tanh_ok")
        k_sum_ok = sem("k_sum_ok")
        k_inv_ok = sem("k_inv_ok")
        kv_ok = sem("kv_ok")
        kv_sum_ok = sem("kv_sum_ok")
        kv_gate_ok = sem("kv_gate_ok")
        o_t_ok = sem("o_t_ok")
        attn_in_ps = sem("attn_in_ps")
        res1_ok = sem("res1_ok")
        stats_ok = [sem(f"stats_ok{n}") for n in range(3)]
        mv_ok = [sem(f"mv_ok{n}") for n in range(3)]
        neg_mean_ok = [sem(f"neg_mean_ok{n}") for n in range(3)]
        eps_ok = [sem(f"eps_ok{n}") for n in range(3)]
        rstd_ok = [sem(f"rstd_ok{n}") for n in range(3)]
        shift_ok = [sem(f"shift_ok{n}") for n in range(3)]
        std_ok = [sem(f"std_ok{n}") for n in range(3)]
        last_rstd_ok = [sem(f"last_rstd_ok{n}") for n in range(3)]
        x1_ok = sem("x1_ok")
        x1t_in_ps = sem("x1t_in_ps")
        x1_t_ok = sem("x1_t_ok")
        logit_in_ps = sem("logit_in_ps")
        logits_ok = sem("logits_ok")
        top_ok = sem("top_ok")
        top_i_ok = sem("top_i_ok")
        top_d_ok = sem("top_d_ok")
        th8_ok = sem("th8_ok")
        den8_ok = sem("den8_ok")
        inv8_ok = sem("inv8_ok")
        exp8_ok = sem("exp8_ok")
        sum8_ok = sem("sum8_ok")
        isum8_ok = sem("isum8_ok")
        dp_ok = sem("dp_ok")
        th2_ok = sem("th2_ok")
        w_top_ok = sem("w_top_ok")
        w1_in = [sem(f"w1_in{s}") for s in range(R * TOP_K)]
        w2_in = [sem(f"w2_in{s}") for s in range(R * TOP_K)]
        b2_in = [sem(f"b2_in{s}") for s in range(R * TOP_K)]
        h_in_ps = sem("h_in_ps")
        h_ok = sem("h_ok")
        out_in_ps = sem("out_in_ps")
        last_out_in_ps = sem("last_out_in_ps")
        b2w_ok = sem("b2w_ok")
        b2c_ok = sem("b2c_ok")
        x1_b2_ok = sem("x1_b2_ok")
        x1_beta_ok = sem("x1_beta_ok")
        y0_ok = sem("y0_ok")
        y_ok = sem("y_ok")
        y_last_ok = sem("y_last_ok")
        z_ok = sem("z_ok")
        zg_ok = sem("zg_ok")
        u_ok = sem("u_ok")
        center_ok = sem("center_ok")
        fin_last_ok = sem("fin_last_ok")
        fin_ok = sem("fin_ok")
        out_dma = [sem(f"out_dma{p}") for p in range(2)]

        block = ctx.enter_context(nc.Block())

        def pieces(b):
            return b + 1 if b < GB else b // GB + GB

        @block.sync
        def _(sp):
            for b in range(GB):
                sp.dma_start(xt[:, b * S:(b + 1) * S], xt_d[:, b * S:(b + 1) * S]).then_inc(in_xt[b], 16)
            for g in range(1, G):
                sp.dma_start(xt[:, g * GS:(g + 1) * GS], xt_d[:, g * GS:(g + 1) * GS]
                             ).then_inc(in_xt[pieces(GB * g) - 1], 16)
                if g == 1:
                    sp.dma_start(x_tok[:, 0:GB * NT, :], x_d[0:GB].rearrange("b (j t) d -> t (b j) d", t=128)).then_inc(in_x[0], 16)
                    sp.dma_start(wr[:, :], wr_d).then_inc(in_small, 16)
                    sp.dma_start(rows[:, :], rows_d.partition_broadcast(128)).then_inc(in_small, 16)
                    sp.dma_start(ident[:, :], ident_d).then_inc(in_small, 16)
            sp.dma_start(x_tok[:, GB * NT:, :], x_d[GB:].rearrange("b (j t) d -> t (b j) d", t=128)).then_inc(in_x[1], 16)

            def fetch(b):
                sp.wait_ge(top_i_ok, b + 1)
                if b >= R:
                    sp.wait_ge(out_in_ps, TOP_K * (b - R + 1))
                    sp.wait_ge(x1_b2_ok, b - R + 1)
                expert = []
                for k in range(TOP_K):
                    s = TOP_K * (b % R) + k
                    expert.append(sp.value_load(top_i[b % R][0:1, k:k + 1], min_val=0, max_val=E - 1))
                    sp.dma_start(w1b[s][:, :], w1b_d[bass.ds(expert[k], 1), :, :].rearrange("e p n -> (e p) n")
                                 ).then_inc(w1_in[s], 16)
                for k, e in enumerate(expert):
                    s = TOP_K * (b % R) + k
                    sp.dma_start(w2[s][:, :, :].rearrange("p c d -> p (c d)"),
                                 w2_d[bass.ds(e, 1), :, :].rearrange("e p n -> (e p) n")).then_inc(w2_in[s], 16)
                    sp.dma_start(b2[s][:, :], b2_d[bass.ds(e, 1), :].partition_broadcast(128)
                                 .rearrange("p e d -> p (e d)")).then_inc(b2_in[s], 16)

            def store(b):
                if b < B - 1:
                    sp.wait_ge(fin_ok, b + 1)
                else:
                    sp.wait_ge(fin_last_ok, 1)
                sp.dma_start(out_d[b, :, :].rearrange("(j t) d -> t j d", t=128),
                             fin[b % 2][:, :, :]).then_inc(out_dma[b % 2], 16)

            for b in range(B):
                fetch(b)
                if b >= 3:
                    store(b - 3)
            for b in range(B - 3, B):
                store(b)
            for p in range(2):
                sp.wait_ge(out_dma[p], 16 * (B // 2))

        @block.tensor
        def _(pe):
            def project_first(b, n, ready):
                pe.wait_ge(in_xt[b], 16)
                pe.matmul(first_kvq_ps[b][n], wkvqc[:, n * D:(n + 1) * D], xt[:, b * S:(b + 1) * S], start=True,
                          stop=True).then_inc(ready, 1)

            def project(g, n, ready, read):
                if g >= 2:
                    pe.wait_ge(read, pieces(GB * (g - 2) + 1))
                pe.wait_ge(in_xt[pieces(GB * g) - 1], 16)
                pe.matmul(kvq_ps[g % 2][n][:, :], wkvqc[:, n * D:(n + 1) * D], xt[:, g * GS:(g + 1) * GS],
                          start=True, stop=True).then_inc(ready, 1)

            def project_k(g):
                project(g, 0, k_in_ps, k_exp_ok)

            def project_v(g):
                project(g, 1, v_in_ps, v_ok)

            def project_q(g):
                project(g, 2, q_in_ps, q_tanh_ok)

            def keep_warm(n):
                for _ in range(n):
                    pe.matmul(warm_ps, ones[:, 0:128], ones[:, :], start=True, stop=True)

            def attn_out(b):
                pe.wait_ge(o_t_ok, b + 1)
                if b == 0:
                    pe.wait_ge(wc_ok, 1)
                else:
                    pe.wait_ge(res1_ok, b)
                for t in range(NT):
                    mm = pe.matmul(attn_ps[:, t * D:(t + 1) * D], o_t[b % R][:, t * 128:(t + 1) * 128], wc_half[:, :],
                                   start=True, stop=True)
                mm.then_inc(attn_in_ps, 1)

            def transpose_x1(b):
                pe.wait_ge(x1_ok, b + 1)
                if b == 0:
                    pe.wait_ge(in_small, 48)
                else:
                    pe.wait_ge(logits_ok, b)
                for t in range(NT):
                    mm = pe.transpose(x1t_ps[:, t * 128:(t + 1) * 128], x1[b % R][:, t, :], ident[:, :])
                mm.then_inc(x1t_in_ps, 1)

            def router(b):
                pe.wait_ge(x1_t_ok, b + 1)
                pe.matmul(logit_ps, x1_sum[b % R][:, 0:1].to_broadcast([D, 128]), wr[:, :], start=True,
                          stop=True).then_inc(logit_in_ps, 1)

            def up(b, k, chunks=range(NF)):
                s = TOP_K * (b % R) + k
                if 0 in chunks:
                    pe.wait_ge(w1_in[s], 16 * (b // R + 1))
                    if b == 0:
                        pe.wait_ge(v_ok, pieces(GB * (G - 2 + k)))
                    else:
                        pe.wait_ge(h_ok, TOP_K * (b - 1) + k + 1)
                for c in chunks:
                    mm = pe.matmul(h_ps[k][c // 2][:, (c % 2) * S:(c % 2 + 1) * S], w1b[s][:, c * D:(c + 1) * D],
                                   x1_t[b % R][:, :], start=True, stop=True)
                    if c % 2:
                        mm.then_inc(h_in_ps, 1)

            def down(b, k):
                s = TOP_K * (b % R) + k
                pe.wait_ge(w2_in[s], 16 * (b // R + 1))
                pe.wait_ge(h_ok, TOP_K * b + k + 1)
                if k == 0 and b < 2:
                    pe.wait_ge(q_tanh_ok, pieces(GB * (G - 2 + b)))
                if k == 0 and b >= 2:
                    pe.wait_ge(y_ok, b - 1)
                for t in range(NT):
                    for c in range(NF):
                        mm = pe.matmul(out_ps[b % 2][:, k * S + t * D:k * S + (t + 1) * D],
                                       h_t[k][:, c, t * 128:(t + 1) * 128], w2[s][:, c, :],
                                       start=(c == 0), stop=(c == NF - 1))
                mm.then_inc(out_in_ps, 1)

            def down_last(b):
                k = TOP_K - 1
                s = TOP_K * (b % R) + k
                pe.wait_ge(w2_in[s], 16 * (b // R + 1))
                pe.wait_ge(h_ok, TOP_K * (b + 1))
                pe.wait_ge(y_ok, b)
                for t in range(NT):
                    for c in range(NF):
                        mm = pe.matmul(last_out_ps[t], h_t[k][:, c, t * 128:(t + 1) * 128], w2[s][:, c, :],
                                       start=(c == 0), stop=(c == NF - 1))
                    mm.then_inc(last_out_in_ps, 1)

            pe.wait_ge(const_ok, 1)
            keep_warm(WARM)
            pe.wait_ge(in_k, 16)
            project_first(0, 0, k_in_ps)
            pe.wait_ge(in_vqc, 16)
            project_first(0, 1, v_in_ps)
            project_first(0, 2, q_in_ps)
            project_first(1, 0, k_in_ps)
            project_first(1, 1, v_in_ps)
            pe.wait_ge(q_tanh_ok, 1)
            project_first(1, 2, q_in_ps)
            project_k(1)
            attn_out(0)
            project_v(1)
            project_q(1)
            project_k(2)
            project_v(2)
            transpose_x1(0)
            project_k(3)
            router(0)
            attn_out(1)
            project_q(2)
            project_v(3)
            attn_out(2)
            project_q(3)
            transpose_x1(1)
            up(0, 0, range(0, NF // 2))
            router(1)
            up(0, 0, range(NF // 2, NF))
            for b in range(B):
                if 0 < b and b + 2 < B:
                    transpose_x1(b + 2)
                up(b, 1)
                if b == 0:
                    transpose_x1(b + 2)
                if b + 3 < B:
                    attn_out(b + 3)
                down(b, 0)
                if b + 2 < B:
                    router(b + 2)
                if b + 1 < B:
                    up(b + 1, 0)
                if b < B - 1:
                    down(b, 1)
            down_last(B - 1)

        @block.scalar
        def _(act):
            act.dma_start(wkvqc[:, 0:D], wkvqc_d[:, 0:D]).then_inc(in_k, 16)
            act.dma_start(wkvqc[:, D:4 * D], wkvqc_d[:, D:4 * D]).then_inc(in_vqc, 16)

            def columns_and_source(p, n):
                if p < GB:
                    return slice(p * S, (p + 1) * S), first_kvq_ps[p][n]
                g = p - GB + 1
                return slice(g * GS, (g + 1) * GS), kvq_ps[g % 2][n][:, :]

            def exp_k(p):
                act.wait_ge(k_in_ps, p + 1)
                to, source = columns_and_source(p, 0)
                nc.scalar.activation(k_exp[:, to], source, ACT.Exp).then_inc(k_exp_ok, 1)

            def copy_v(p):
                act.wait_ge(v_in_ps, p + 1)
                to, source = columns_and_source(p, 1)
                nc.scalar.copy(v_sb[:, to], source).then_inc(v_ok, 1)

            def tanh_q(p):
                act.wait_ge(q_in_ps, p + 1)
                to, source = columns_and_source(p, 2)
                nc.scalar.activation(q_tanh[:, to], source, ACT.Tanh, scale=0.5).then_inc(q_tanh_ok, 1)

            def norm(n, src, dst, b, done):
                act.wait_ge(shift_ok[n], b + 1)
                for t in range(NT):
                    a = nc.scalar.activation(dst[:, t, :], src[:, t, :], ACT.Identity, bias=shift[n][b % R][:, t:t + 1],
                                             scale=rstd[n][b % R][:, t:t + 1])
                a.then_inc(done, 1)

            def norm1(b):
                if b >= R:
                    act.wait_ge(x1_beta_ok, b - R + 1)
                norm(0, res1[b % R], x1[b % R], b, x1_ok)

            def evacuate_x1t(b):
                act.wait_ge(x1t_in_ps, b + 1)
                nc.scalar.activation(x1_t[b % R][:, :], x1t_ps, ACT.Identity,
                                     accum_out=x1_sum[b % R][:, :]).then_inc(x1_t_ok, 1)

            def gelu(b, k):
                q = TOP_K * b + k
                if b >= 1:
                    act.wait_ge(out_in_ps, q - 1)
                for c in range(NF):
                    if c % 2 == 0:
                        act.wait_ge(h_in_ps, NF // 2 * q + c // 2 + 1)
                    a = nc.scalar.activation(h_t[k][:, c, :], h_ps[k][c // 2][:, (c % 2) * S:(c % 2 + 1) * S],
                                             ACT.Gelu, bias=w1b[TOP_K * (b % R) + k][:, F + c:F + c + 1])
                a.then_inc(h_ok, 1)

            def router_tanh8(b):
                act.wait_ge(top_d_ok, b + 1)
                nc.scalar.activation(th8[b % R][:, :], top_d[b % R][:, :], ACT.Tanh, scale=0.5).then_inc(th8_ok, 1)

            def router_tanh2(b):
                act.wait_ge(dp_ok, b + 1)
                nc.scalar.activation(th2[b % R][:, :], dp[b % R][:, :], ACT.Tanh, scale=0.5).then_inc(th2_ok, 1)

            def root(n, b):
                act.wait_ge(mv_ok[n], NT * (b + 1))
                nc.scalar.activation(std[n][:, :], mv[n][b % R][:, :, 1], ACT.Sqrt, bias=eps_col[:, :]
                                     ).then_inc(std_ok[n], 1)

            def norm2(b):
                norm(1, y[b % 2], z, b, z_ok)

            def norm3(b):
                if b >= 2:
                    act.wait_ge(out_dma[b % 2], 16 * (b // 2))
                norm(2, u[b % 2], fin[b % 2], b, fin_ok)

            for p in range(P - 2):
                exp_k(p)
                copy_v(p)
                tanh_q(p)
            exp_k(P - 2)
            norm1(0)
            copy_v(P - 2)
            evacuate_x1t(0)
            exp_k(P - 1)
            act.wait_ge(const_ok, 3)
            nc.scalar.activation(gelu_warm[:, :], ones[:, 0:1], ACT.Gelu)
            tanh_q(P - 2)
            copy_v(P - 1)
            norm1(1)
            tanh_q(P - 1)
            evacuate_x1t(1)
            router_tanh8(0)
            gelu(0, 0)
            norm1(2)
            router_tanh8(1)
            for b in range(B + 1):
                if 0 < b and b + 2 < B:
                    evacuate_x1t(b + 2)
                if b == B - 1:
                    router_tanh2(b)
                if b < B:
                    gelu(b, 1)
                if 1 < b < B - 1:
                    norm3(b - 2)
                if b == 0:
                    evacuate_x1t(b + 2)
                if b < B - 1:
                    router_tanh2(b)
                if 0 < b and b - 1 < DVE_NORM2:
                    norm2(b - 1)
                if b > 1 and b == B - 1:
                    norm3(b - 2)
                    nc.scalar.activation(sqrt_warm[:, :], ones[:, 0:1], ACT.Sqrt)
                if b == B:
                    root(1, b - 1)
                    norm3(b - 2)
                    root(2, b - 1)
                if b + 3 < B:
                    norm1(b + 3)
                if b + 1 < B:
                    gelu(b + 1, 0)
                if b + 2 < B:
                    router_tanh8(b + 2)

        @block.vector
        def _(dve):
            def cols(a, b):
                return a[:, b * S:(b + 1) * S]

            def sum_keys(b):
                dve.wait_ge(k_exp_ok, pieces(b))
                nc.vector.tensor_tensor_scan(k_sum[b % R][:, :], ones[:, :], cols(k_exp, b), ATTN_EPS, ALU.mult,
                                             ALU.add).then_inc(k_sum_ok, 1)

            def invert_keys(b):
                dve.wait_ge(k_sum_ok, b + 1)
                nc.vector.reciprocal(k_inv[b % R][:, :], k_sum[b % R][:, :]).then_inc(k_inv_ok, 1)

            def sum_kv(b):
                dve.wait_ge(kv_ok, b + 1)
                nc.vector.tensor_tensor_scan(kv_sum[b % R][:, :], ones[:, :], kv[b % R][:, :], 0.0, ALU.mult,
                                             ALU.add).then_inc(kv_sum_ok, 1)

            def gate_kv(b):
                dve.wait_ge(q_tanh_ok, pieces(b))
                dve.wait_ge(kv_sum_ok, b + 1)
                nc.vector.scalar_tensor_tensor(out=kv_gate[b % R][:, :], in0=cols(q_tanh, b), scalar=1.0,
                                               in1=kv_sum[b % R][:, :], op0=ALU.add,
                                               op1=ALU.mult).then_inc(kv_gate_ok, 1)

            def attend(b):
                dve.wait_ge(kv_gate_ok, b + 1)
                dve.wait_ge(k_inv_ok, b + 1)
                nc.vector.tensor_tensor(o_t[b % R][:, :], kv_gate[b % R][:, :], k_inv[b % R][:, :],
                                        ALU.mult).then_inc(o_t_ok, 1)

            def add_x(b):
                dve.wait_ge(attn_in_ps, b + 1)
                dve.wait_ge(in_x[0 if b < GB else 1], 16)
                nc.vector.tensor_tensor(res1[b % R][:, :, :], attn_ps.rearrange("p (j d) -> p j d", d=D),
                                        x_tok[:, b * NT:(b + 1) * NT, :], ALU.add).then_inc(res1_ok, 1)

            def tile_stats(n, src, b, ready):
                dve.wait_ge(ready, b + 1)
                for t in range(NT):
                    nc.vector.bn_stats(stats[n][b % R][:, t, :], src[:, t, :]).then_inc(stats_ok[n], 1)

            def aggregate(n, b):
                for t in range(NT):
                    dve.wait_ge(stats_ok[n], NT * b + t + 1)
                    nc.vector.bn_aggr(mv[n][b % R][:, t, :], stats[n][b % R][:, t, :]).then_inc(mv_ok[n], 1)

            def prepare_norm(n, b):
                dve.wait_ge(mv_ok[n], NT * (b + 1))
                nc.vector.tensor_scalar(var_eps[n][b % R][:, :], mv[n][b % R][:, :, 1], LN_EPS, None, ALU.add).then_inc(eps_ok[n], 1)
                negate_mean(n, b)

            def add_br(b):
                dve.wait_ge(logit_in_ps, b + 1)
                nc.vector.scalar_tensor_tensor(out=logits[b % R][:, :], in0=logit_ps, scalar=1.0 / S, in1=br_row,
                                               op0=ALU.mult, op1=ALU.add).then_inc(logits_ok, 1)

            def sort_logits(b):
                dve.wait_ge(logits_ok, b + 1)
                nc.vector.max(top[b % R][:, :], logits[b % R][:, :]).then_inc(top_ok, 1)

            def find_experts(b):
                dve.wait_ge(top_ok, b + 1)
                nc.vector.max_index(top_i[b % R][:, :], top[b % R][:, :], logits[b % R][:, :]).then_inc(top_i_ok, 1)

            def below_top(b):
                nc.vector.tensor_scalar(top_d[b % R][:, :], top[b % R][:, :], top[b % R][:, 0:1], None,
                                        ALU.subtract).then_inc(top_d_ok, 1)

            def exp_denominator(b):
                dve.wait_ge(th8_ok, b + 1)
                nc.vector.tensor_scalar(den8[b % R][:, :], th8[b % R][:, :], -1.0, 1.0, ALU.mult,
                                        ALU.add).then_inc(den8_ok, 1)

            def exp_inverse(b):
                dve.wait_ge(den8_ok, b + 1)
                nc.vector.reciprocal(inv8[b % R][:, :], den8[b % R][:, :]).then_inc(inv8_ok, 1)

            def exp_value(b):
                dve.wait_ge(inv8_ok, b + 1)
                nc.vector.tensor_scalar(exp8[b % R][:, :], inv8[b % R][:, :], 2.0, -1.0, ALU.mult,
                                        ALU.add).then_inc(exp8_ok, 1)

            def exp_sum(b):
                dve.wait_ge(exp8_ok, b + 1)
                nc.vector.tensor_reduce(sum8[b % R][:, :], exp8[b % R][:, :], AX.X, ALU.add).then_inc(sum8_ok, 1)

            def exp_sum_inverse(b):
                dve.wait_ge(sum8_ok, b + 1)
                nc.vector.reciprocal(isum8[b % R][:, :], sum8[b % R][:, :]).then_inc(isum8_ok, 1)

            def top_two_apart(b):
                dve.wait_ge(isum8_ok, b + 1)
                nc.vector.scalar_tensor_tensor(out=dp[b % R][:, :], in0=exp8[b % R][:, 0:1],
                                               scalar=exp8[b % R][:, 1:2], in1=isum8[b % R][:, :],
                                               op0=ALU.subtract, op1=ALU.mult).then_inc(dp_ok, 1)

            def top_weights(b):
                dve.wait_ge(th2_ok, b + 1)
                nc.vector.tensor_scalar(w_top[b % R][:, 0:1], th2[b % R][:, :], 0.5, 0.5, ALU.mult, ALU.add)
                nc.vector.tensor_scalar(w_top[b % R][:, 1:2], th2[b % R][:, :], -0.5, 0.5, ALU.mult,
                                        ALU.add).then_inc(w_top_ok, 1)

            def combine_first(b):
                dve.wait_ge(x1_b2_ok, b + 1)
                dve.wait_ge(out_in_ps, TOP_K * (b + 1) if b < B - 1 else TOP_K * b + 1)
                nc.vector.scalar_tensor_tensor(out=y0[:, :, :], in0=expert_out(b, 0), scalar=w_top[b % R][:, 0:1],
                                               in1=x1_b2[b % R][:, :, :], op0=ALU.mult,
                                               op1=ALU.add).then_inc(y0_ok, 1)

            def combine_second(b):
                dve.wait_ge(y0_ok, b + 1)
                nc.vector.scalar_tensor_tensor(out=y[b % 2][:, :, :], in0=expert_out(b, 1),
                                               scalar=w_top[b % R][:, 1:2], in1=y0[:, :, :], op0=ALU.mult,
                                               op1=ALU.add).then_inc(y_ok, 1)

            def combine_last(b, t):
                dve.wait_ge(y0_ok, b + 1)
                dve.wait_ge(last_out_in_ps, t + 1)
                nc.vector.scalar_tensor_tensor(out=y[b % 2][:, t, :], in0=last_out_ps[t], scalar=w_top[b % R][:, 1:2],
                                               in1=y0[:, t, :], op0=ALU.mult, op1=ALU.add).then_inc(y_last_ok, 1)

            def stats_last(b, t):
                dve.wait_ge(y_last_ok, t + 1)
                nc.vector.bn_stats(stats[1][b % R][:, t, :], y[b % 2][:, t, :]).then_inc(stats_ok[1], 1)

            def expert_out(b, k):
                return out_ps[b % 2][:, k * S:(k + 1) * S].rearrange("p (j d) -> p j d", d=D)

            def add_x1(b):
                dve.wait_ge(zg_ok, b + 1)
                nc.vector.tensor_tensor(u[b % 2][:, :, :], zg[:, :, :], x1_beta[b % R][:, :, :],
                                        ALU.add).then_inc(u_ok, 1)

            def invert_root(n):
                dve.wait_ge(std_ok[n], 1)
                nc.vector.reciprocal(last_rstd[n][:, :], std[n][:, :]).then_inc(last_rstd_ok[n], 1)

            def negate_mean(n, b):
                nc.vector.tensor_scalar(neg_mean[n][b % R][:, :], mv[n][b % R][:, :, 0], -1.0, None,
                                        ALU.mult).then_inc(neg_mean_ok[n], 1)

            def center_last(b):
                dve.wait_ge(neg_mean_ok[1], b + 1)
                for t in range(NT):
                    if b == B - 1 and t == 1:
                        invert_root(1)
                    c = nc.vector.scalar_tensor_tensor(out=z[:, t, :], in0=y[b % 2][:, t, :],
                                                       scalar=neg_mean[1][b % R][:, t:t + 1], in1=gamma_row,
                                                       op0=ALU.add, op1=ALU.mult)
                c.then_inc(center_ok, 1)

            def scale_last(b):
                dve.wait_ge(center_ok, b - DVE_NORM2 + 1)
                dve.wait_ge(x1_beta_ok, b + 1)
                if b < B - 1:
                    dve.wait_ge(rstd_ok[1], b + 1)
                    scale = rstd[1][b % R]
                else:
                    dve.wait_ge(last_rstd_ok[1], 1)
                    scale = last_rstd[1]
                dve.wait_ge(fin_ok, b - 1)
                for t in range(NT):
                    c = nc.vector.scalar_tensor_tensor(out=u[b % 2][:, t, :], in0=z[:, t, :],
                                                       scalar=scale[:, t:t + 1],
                                                       in1=x1_beta[b % R][:, t, :], op0=ALU.mult, op1=ALU.add)
                c.then_inc(u_ok, 1)

            def finish_last(b):
                dve.wait_ge(last_rstd_ok[2], 1)
                dve.wait_ge(neg_mean_ok[2], b + 1)
                dve.wait_ge(out_dma[b % 2], 16 * (b // 2))
                for t in range(NT):
                    c = nc.vector.tensor_scalar(fin[b % 2][:, t, :], u[b % 2][:, t, :], neg_mean[2][b % R][:, t:t + 1],
                                                last_rstd[2][:, t:t + 1], ALU.add, ALU.mult)
                c.then_inc(fin_last_ok, 1)

            nc.vector.memset(ones[:, :], 1.0).then_inc(const_ok, 1)
            nc.vector.memset(eps_col[:, :], LN_EPS).then_inc(const_ok, 1)
            nc.vector.memset(neg_half[:, :], -0.5).then_inc(const_ok, 1)
            dve.wait_ge(in_vqc, 16)
            nc.vector.tensor_scalar(wc_half[:, :], wkvqc[:, 3 * D:4 * D], 0.5, None, ALU.mult).then_inc(wc_ok, 1)
            dve.wait_ge(const_ok, 3)
            sum_keys(0)
            invert_keys(0)
            sum_kv(0)
            gate_kv(0)
            attend(0)
            sum_keys(1)
            sum_kv(1)
            sum_keys(2)
            add_x(0)
            tile_stats(0, res1[0], 0, res1_ok)
            aggregate(0, 0)
            prepare_norm(0, 0)
            gate_kv(1)
            invert_keys(1)
            attend(1)
            invert_keys(2)
            dve.wait_ge(in_small, 48)
            add_br(0)
            sum_kv(2)
            sort_logits(0)
            add_x(1)
            find_experts(0)
            tile_stats(0, res1[1], 1, res1_ok)
            gate_kv(2)
            aggregate(0, 1)
            below_top(0)
            prepare_norm(0, 1)
            attend(2)
            sum_kv(3)
            sum_keys(3)
            add_x(2)
            tile_stats(0, res1[2], 2, res1_ok)
            aggregate(0, 2)
            gate_kv(3)
            prepare_norm(0, 2)
            sum_keys(4)
            exp_denominator(0)
            add_br(1)
            exp_inverse(0)
            sort_logits(1)
            exp_value(0)
            find_experts(1)
            below_top(1)
            exp_sum(0)
            invert_keys(3)
            attend(3)
            for b in range(B + 1):
                last, now, soon, attn, far = b - 1, b, b + 2, b + 3, b + 4
                if now == B - 1:
                    exp_sum_inverse(now)
                    top_two_apart(now)
                if b > 0:
                    combine_first(last)
                if now < B - 1:
                    exp_sum_inverse(now)
                if now == B - 1:
                    top_weights(now)
                if 0 < b < B:
                    combine_second(last)
                if now < B - 1:
                    top_two_apart(now)
                if 0 < b < B:
                    tile_stats(1, y[last % 2], last, y_ok)
                    aggregate(1, last)
                if 0 < b and far < B:
                    sum_keys(far)
                if now == B:
                    combine_last(last, 0)
                    stats_last(last, 0)
                    tile_stats(2, u[(last - 1) % 2], last - 1, u_ok)
                    combine_last(last, 1)
                    aggregate(2, last - 1)
                    stats_last(last, 1)
                    aggregate(1, last)
                    prepare_norm(2, last - 1)
                if 0 < b < B:
                    prepare_norm(1, last)
                if now == B:
                    dve.wait_ge(mv_ok[1], NT * B)
                    negate_mean(1, last)
                if attn < B:
                    add_x(attn)
                if attn < B:
                    tile_stats(0, res1[attn % R], attn, res1_ok)
                    aggregate(0, attn)
                if now < B - 1:
                    top_weights(now)
                if attn < B:
                    prepare_norm(0, attn)
                if far < B:
                    invert_keys(far)
                if soon < B:
                    add_br(soon)
                if far < B:
                    sum_kv(far)
                if soon < B:
                    sort_logits(soon)
                if b + 1 < B:
                    exp_denominator(b + 1)
                if soon < B:
                    find_experts(soon)
                    below_top(soon)
                if 0 < b and last < DVE_NORM2:
                    add_x1(last)
                if last >= DVE_NORM2:
                    center_last(last)
                    scale_last(last)
                if b + 1 < B:
                    exp_inverse(b + 1)
                if far < B:
                    gate_kv(far)
                if 0 < b != B - 1:
                    tile_stats(2, u[last % 2], last, u_ok)
                    aggregate(2, last)
                if b + 1 < B:
                    exp_value(b + 1)
                if far < B:
                    attend(far)
                if 0 < b < B - 1:
                    prepare_norm(2, last)
                if now == B:
                    dve.wait_ge(mv_ok[2], NT * B)
                    negate_mean(2, last)
                    invert_root(2)
                if b + 1 < B:
                    exp_sum(b + 1)
            finish_last(B - 1)

        @block.gpsimd
        def _(pool):
            def k_times_v(b):
                pool.wait_ge(k_exp_ok, pieces(b))
                pool.wait_ge(v_ok, pieces(b))
                if b >= R:
                    pool.wait_ge(kv_sum_ok, b - R + 1)
                nc.gpsimd.tensor_tensor(kv[b % R][:, :], k_exp[:, b * S:(b + 1) * S], v_sb[:, b * S:(b + 1) * S],
                                        ALU.mult).then_inc(kv_ok, 1)

            def rsqrt(n, b):
                pool.wait_ge(eps_ok[n], b + 1)
                nc.gpsimd.tensor_tensor(rstd[n][b % R][:, :], var_eps[n][b % R][:, :], neg_half[:, :], ALU.pow).then_inc(rstd_ok[n], 1)
                pool.wait_ge(neg_mean_ok[n], b + 1)
                pool.wait_ge(rstd_ok[n], b + 1)
                nc.gpsimd.tensor_tensor(shift[n][b % R][:, :], neg_mean[n][b % R][:, :], rstd[n][b % R][:, :],
                                        ALU.mult).then_inc(shift_ok[n], 1)

            def weigh_b2(b):
                pool.wait_ge(w_top_ok, b + 1)
                for k in range(TOP_K):
                    s = TOP_K * (b % R) + k
                    pool.wait_ge(b2_in[s], 16 * (b // R + 1))
                    m = nc.gpsimd.tensor_scalar(b2w[k][:, :], b2[s][:, :], w_top[b % R][:, k:k + 1], 1.0, ALU.mult,
                                                ALU.mult)
                m.then_inc(b2w_ok, 1)
                pool.wait_ge(b2w_ok, b + 1)
                nc.gpsimd.tensor_tensor(b2c[:, :], b2w[0][:, :], b2w[1][:, :], ALU.add).then_inc(b2c_ok, 1)

            def add_b2(b):
                pool.wait_ge(b2c_ok, b + 1)
                pool.wait_ge(x1_ok, b + 1)
                nc.gpsimd.tensor_tensor(x1_b2[b % R][:, :, :], x1[b % R][:, :, :],
                                        b2c[:, :].unsqueeze(1).to_broadcast([128, NT, D]), ALU.add
                                        ).then_inc(x1_b2_ok, 1)

            def add_beta(b):
                pool.wait_ge(x1_ok, b + 1)
                nc.gpsimd.tensor_tensor(x1_beta[b % R][:, :, :], x1[b % R][:, :, :],
                                        beta_row.unsqueeze(1).to_broadcast([128, NT, D]), ALU.add
                                        ).then_inc(x1_beta_ok, 1)

            def scale_gamma(b):
                pool.wait_ge(z_ok, b + 1)
                nc.gpsimd.tensor_tensor(zg[:, :, :], z[:, :, :], gamma_row.unsqueeze(1).to_broadcast([128, NT, D]),
                                        ALU.mult).then_inc(zg_ok, 1)

            k_times_v(0)
            k_times_v(1)
            pool.wait_ge(const_ok, 3)
            rsqrt(0, 0)
            k_times_v(2)
            k_times_v(3)
            rsqrt(0, 1)
            pool.wait_ge(in_small, 48)
            rsqrt(0, 2)
            for b in range(B + 1):
                if b + 4 < B:
                    k_times_v(b + 4)
                if b == B - 1:
                    weigh_b2(b)
                if 0 < b < B:
                    rsqrt(1, b - 1)
                if b == B - 1:
                    add_b2(b)
                if b < B - 1:
                    add_beta(b)
                if 0 < b and b - 1 < DVE_NORM2:
                    scale_gamma(b - 1)
                if b + 3 < B:
                    rsqrt(0, b + 3)
                if b < B - 1:
                    weigh_b2(b)
                    add_b2(b)
                if b == B - 1:
                    add_beta(b)
                if b == B:
                    rsqrt(2, b - 2)
                if 0 < b < B - 1:
                    rsqrt(2, b - 1)


def kernel(**inputs):
    import numpy as _np
    import concourse.bacc as _bacc
    from concourse.bass_utils import run_bass_kernel_spmd as _run

    X = _np.asarray(inputs["L0_attn_X"])
    W1, W2 = _np.asarray(inputs["L0_ffn_W1"]), _np.asarray(inputs["L0_ffn_W2"])
    B, S, D = X.shape
    E, _, F = W1.shape
    NF = F // D
    row = lambda *names: [_np.asarray(inputs[n]).reshape(1, -1) for n in names]
    arrays = {
        "xt": X.transpose(2, 0, 1).reshape(D, B * S),
        "x": X,
        "wkvqc": _np.concatenate([_np.asarray(inputs["L0_attn_W" + n]) for n in "kvqc"], axis=1),
        "w1b": _np.concatenate([W1, _np.asarray(inputs["L0_ffn_b1"]).reshape(E, NF, D).transpose(0, 2, 1)], axis=2),
        "w2": W2.reshape(E, NF, D, D).transpose(0, 2, 1, 3).reshape(E, D, NF * D),
        "b2": _np.asarray(inputs["L0_ffn_b2"]),
        "wr": _np.asarray(inputs["L0_ffn_Wr"]),
        "rows": _np.concatenate(row("L0_ffn_br", "L0_ffn_gamma", "L0_ffn_beta"), axis=1),
        "ident": _np.eye(128, dtype=_np.float32),
    }
    arrays = {n: _np.ascontiguousarray(a) for n, a in arrays.items()}
    nc = _bacc.Bacc("TRN2", target_bir_lowering=False, num_devices=1)
    aps = [nc.dram_tensor("in_" + n, a.shape, F32, kind="ExternalInput").ap() for n, a in arrays.items()]
    out = nc.dram_tensor("out", X.shape, F32, kind="ExternalOutput").ap()
    attention_free_moe_block(nc, *aps, out)
    r = _run(nc, [{"in_" + n: a for n, a in arrays.items()}], core_ids=[0])
    return r.results[0]["out"]
```
